# Optimizing a Trainium2 kernel written in Bass

```python
import numpy as np
import jax
import jax.numpy as jnp

def _softmax(x, axis=-1):
    return jax.nn.softmax(x, axis=axis)

def _gelu(x):
    return jax.nn.gelu(x, approximate=True)

def _silu(x):
    return jax.nn.silu(x)

def _sigmoid(x):
    return jax.nn.sigmoid(x)

def _layernorm(x, axis=-1, eps=1e-05):
    m = jnp.mean(x, axis=axis, keepdims=True)
    v = jnp.var(x, axis=axis, keepdims=True)
    return (x - m) / jnp.sqrt(v + eps)

def _scatter_add(tgt, idx, src, axis=0):
    return tgt.at[idx].add(src)

def _segment_sum(src, seg, n):
    return jax.ops.segment_sum(src, seg, n)
kernel_name = 'mk_recurrent_d1_jaxref_r4_ae5cce'

def setup_inputs(seed: int=0):
    np.random.seed(seed)
    _w = jnp.asarray

    def _L0_attn_setup():
        import jax, jax.numpy as jnp
        import numpy as np
        NUM_HEAD = 16
        D_Q = 128
        D_KV = 128
        ROPE_BASE = 10000.0

        def _cos_sin(seq_len, dim):
            pos = jnp.arange(seq_len, dtype=jnp.float32)[:, None]
            ids = jnp.arange(dim // 2, dtype=jnp.float32)
            theta = ROPE_BASE ** (-2.0 * ids) / (dim // 2)
            r = pos * theta[None, :]
            return (jnp.cos(r), jnp.sin(r))

        def _rope(x, cos, sin):
            b, s, d = x.shape
            xv = x.reshape(b, s, d // 2, 2)
            x0, x1 = (xv[..., 0], xv[..., 1])
            out = jnp.stack([x0 * cos - x1 * sin, x1 * cos + x0 * sin], axis=-1)
            return out.reshape(b, s, d)
        key = jax.random.key(seed)
        ks = jax.random.split(key, 10)
        d_model, d_q, d_kv = (256, D_Q, D_KV)
        b, s = (2, 512)
        w = lambda k, i, o: jax.random.normal(k, (i, o), dtype=jnp.float32) * 0.02
        return {'x': jax.random.normal(ks[0], (b, s, d_model), dtype=jnp.float32), 'Wd_q_w': w(ks[1], d_model, d_q), 'Wd_q_b': jnp.zeros((d_q,), jnp.float32), 'Wu_q_w': w(ks[2], d_q, d_model), 'Wu_q_b': jnp.zeros((d_model,), jnp.float32), 'Wq_r_w': w(ks[3], d_q, d_model), 'Wq_r_b': jnp.zeros((d_model,), jnp.float32), 'Wk_r_w': w(ks[4], d_model, d_model), 'Wk_r_b': jnp.zeros((d_model,), jnp.float32), 'Wd_kv_w': w(ks[5], d_model, d_kv), 'Wd_kv_b': jnp.zeros((d_kv,), jnp.float32), 'Wu_k_w': w(ks[6], d_kv, d_model), 'Wu_k_b': jnp.zeros((d_model,), jnp.float32), 'Wu_v_w': w(ks[7], d_kv, d_model), 'Wu_v_b': jnp.zeros((d_model,), jnp.float32), 'Wo_w': w(ks[8], d_model, d_model), 'Wo_b': jnp.zeros((d_model,), jnp.float32)}
    _L0_attn_in = _L0_attn_setup()

    def _L0_ffn_setup():
        import jax, jax.numpy as jnp
        import numpy as np
        EPS = 1e-08

        def _ternary_linear(x, w):
            alpha = jnp.mean(jnp.abs(w))
            w_t = jnp.sign(w) * (jnp.abs(w) > 0.5 * alpha).astype(w.dtype)
            w_q = w + jax.lax.stop_gradient(w_t - w)
            d = x.shape[-1]
            rms = jnp.sqrt(jnp.sum(x * x, axis=-1, keepdims=True)) / jnp.sqrt(jnp.asarray(d, x.dtype))
            x_norm = x / (rms + EPS)
            return jnp.einsum('bsd,fd->bsf', x_norm, w_q)
        key = jax.random.key(seed)
        k1, k2, k3 = jax.random.split(key, 3)
        d_model, d_ff = (256, 1024)
        B, S = (4, 1024)
        x = jax.random.normal(k1, (B, S, d_model), dtype=jnp.float32)
        w_up = jax.random.normal(k2, (d_ff, d_model), dtype=jnp.float32) * 0.02
        w_down = jax.random.normal(k3, (d_model, d_ff), dtype=jnp.float32) * 0.02
        return {'x': x, 'w_up': w_up, 'w_down': w_down}
    _L0_ffn_in = _L0_ffn_setup()
    _d = {'L0_attn_x': _L0_attn_in['x'], 'L0_attn_Wd_q_w': _L0_attn_in['Wd_q_w'], 'L0_attn_Wd_q_b': _L0_attn_in['Wd_q_b'], 'L0_attn_Wu_q_w': _L0_attn_in['Wu_q_w'], 'L0_attn_Wu_q_b': _L0_attn_in['Wu_q_b'], 'L0_attn_Wq_r_w': _L0_attn_in['Wq_r_w'], 'L0_attn_Wq_r_b': _L0_attn_in['Wq_r_b'], 'L0_attn_Wk_r_w': _L0_attn_in['Wk_r_w'], 'L0_attn_Wk_r_b': _L0_attn_in['Wk_r_b'], 'L0_attn_Wd_kv_w': _L0_attn_in['Wd_kv_w'], 'L0_attn_Wd_kv_b': _L0_attn_in['Wd_kv_b'], 'L0_attn_Wu_k_w': _L0_attn_in['Wu_k_w'], 'L0_attn_Wu_k_b': _L0_attn_in['Wu_k_b'], 'L0_attn_Wu_v_w': _L0_attn_in['Wu_v_w'], 'L0_attn_Wu_v_b': _L0_attn_in['Wu_v_b'], 'L0_attn_Wo_w': _L0_attn_in['Wo_w'], 'L0_attn_Wo_b': _L0_attn_in['Wo_b'], 'L0_ffn_w_up': _L0_ffn_in['w_up'], 'L0_ffn_w_down': _L0_ffn_in['w_down']}
    _x0 = _d['L0_attn_x']
    _d['L0_attn_x'] = jax.random.normal(jax.random.fold_in(jax.random.key(seed), 1), (16, 1024, 256), dtype=_x0.dtype)
    del _x0
    return _d

def reference(L0_attn_x, L0_attn_Wd_q_w, L0_attn_Wd_q_b, L0_attn_Wu_q_w, L0_attn_Wu_q_b, L0_attn_Wq_r_w, L0_attn_Wq_r_b, L0_attn_Wk_r_w, L0_attn_Wk_r_b, L0_attn_Wd_kv_w, L0_attn_Wd_kv_b, L0_attn_Wu_k_w, L0_attn_Wu_k_b, L0_attn_Wu_v_w, L0_attn_Wu_v_b, L0_attn_Wo_w, L0_attn_Wo_b, L0_ffn_w_up, L0_ffn_w_down):

    def _L0_attn_ref(x, Wd_q_w, Wd_q_b, Wu_q_w, Wu_q_b, Wq_r_w, Wq_r_b, Wk_r_w, Wk_r_b, Wd_kv_w, Wd_kv_b, Wu_k_w, Wu_k_b, Wu_v_w, Wu_v_b, Wo_w, Wo_b):
        import jax, jax.numpy as jnp
        import numpy as np
        NUM_HEAD = 16
        D_Q = 128
        D_KV = 128
        ROPE_BASE = 10000.0

        def _cos_sin(seq_len, dim):
            pos = jnp.arange(seq_len, dtype=jnp.float32)[:, None]
            ids = jnp.arange(dim // 2, dtype=jnp.float32)
            theta = ROPE_BASE ** (-2.0 * ids) / (dim // 2)
            r = pos * theta[None, :]
            return (jnp.cos(r), jnp.sin(r))

        def _rope(x, cos, sin):
            b, s, d = x.shape
            xv = x.reshape(b, s, d // 2, 2)
            x0, x1 = (xv[..., 0], xv[..., 1])
            out = jnp.stack([x0 * cos - x1 * sin, x1 * cos + x0 * sin], axis=-1)
            return out.reshape(b, s, d)
        b, s, d_model = x.shape
        h = NUM_HEAD
        hd = d_model // h
        scale = jnp.sqrt(jnp.float32(h + D_KV + D_Q))

        def heads(t):
            return t.reshape(b, s, h, hd).transpose(0, 2, 1, 3)
        cos, sin = _cos_sin(s, d_model)
        ct_q = x @ Wd_q_w + Wd_q_b
        qt_c = heads(ct_q @ Wu_q_w + Wu_q_b)
        qt_r = heads(_rope(ct_q @ Wq_r_w + Wq_r_b, cos, sin))
        query = qt_c + qt_r
        ct_kv = x @ Wd_kv_w + Wd_kv_b
        kt_c = heads(ct_kv @ Wu_k_w + Wu_k_b)
        kt_r = heads(_rope(x @ Wk_r_w + Wk_r_b, cos, sin))
        key = kt_c + kt_r
        value = heads(ct_kv @ Wu_v_w + Wu_v_b)
        attn = jnp.einsum('bhqd,bhkd->bhqk', query, key) / scale
        attn = jax.nn.softmax(attn, axis=-1)
        out = jnp.einsum('bhqk,bhkd->bhqd', attn, value)
        out = out.transpose(0, 2, 1, 3).reshape(b, s, d_model)
        return out @ Wo_w + Wo_b

    def _L0_ffn_ref(x, w_up, w_down):
        import jax, jax.numpy as jnp
        import numpy as np
        EPS = 1e-08

        def _ternary_linear(x, w):
            alpha = jnp.mean(jnp.abs(w))
            w_t = jnp.sign(w) * (jnp.abs(w) > 0.5 * alpha).astype(w.dtype)
            w_q = w + jax.lax.stop_gradient(w_t - w)
            d = x.shape[-1]
            rms = jnp.sqrt(jnp.sum(x * x, axis=-1, keepdims=True)) / jnp.sqrt(jnp.asarray(d, x.dtype))
            x_norm = x / (rms + EPS)
            return jnp.einsum('bsd,fd->bsf', x_norm, w_q)
        h = jax.nn.gelu(_ternary_linear(x, w_up), approximate=False)
        return _ternary_linear(h, w_down)
    x = L0_attn_x
    xn = _layernorm(x, axis=-1)
    s = _L0_attn_ref(xn, L0_attn_Wd_q_w, L0_attn_Wd_q_b, L0_attn_Wu_q_w, L0_attn_Wu_q_b, L0_attn_Wq_r_w, L0_attn_Wq_r_b, L0_attn_Wk_r_w, L0_attn_Wk_r_b, L0_attn_Wd_kv_w, L0_attn_Wd_kv_b, L0_attn_Wu_k_w, L0_attn_Wu_k_b, L0_attn_Wu_v_w, L0_attn_Wu_v_b, L0_attn_Wo_w, L0_attn_Wo_b)
    g = _silu(_L0_ffn_ref(xn, L0_ffn_w_up, L0_ffn_w_down))
    x = x + s * g
    return x

_drawn_inputs = setup_inputs


def setup_inputs(seed=0):
    import zlib

    import numpy as np

    out = dict(_drawn_inputs(seed))
    spreads = {'L0_attn_Wd_q_b': (0.0, 0.8),
     'L0_attn_Wu_q_b': (0.0, 0.8),
     'L0_attn_Wq_r_b': (0.0, 0.8),
     'L0_attn_Wk_r_b': (0.0, 2.0),
     'L0_attn_Wd_kv_b': (0.0, 0.1),
     'L0_attn_Wu_k_b': (0.0, 2.0),
     'L0_attn_Wu_v_b': (0.0, 0.1),
     'L0_attn_Wo_b': (0.0, 0.1)}
    factors = {'L0_attn_Wd_q_w': 8.0,
     'L0_attn_Wu_q_w': 8.0,
     'L0_attn_Wq_r_w': 8.0,
     'L0_attn_Wk_r_w': 8.0,
     'L0_attn_Wd_kv_w': 8.0,
     'L0_attn_Wu_k_w': 8.0}
    for name, (base, spread) in spreads.items():
        noise = np.random.default_rng([zlib.crc32(name.encode()), seed]).standard_normal(out[name].shape)
        drawn = base * np.exp(spread * noise) if base else spread * noise
        out[name] = jnp.asarray(drawn.astype(out[name].dtype))
    for name, factor in factors.items():
        out[name] = (out[name] * factor).astype(out[name].dtype)
    return out
```

```python
from contextlib import ExitStack

import numpy as np

import concourse.bass as bass
from concourse import mybir

F32 = mybir.dt.float32
F16 = mybir.dt.float16
BF16 = mybir.dt.bfloat16
ALU = mybir.AluOpType
ACT = mybir.ActivationFunctionType
AX = mybir.AxisListType

P = 128
S = 1024
D = 256
H = 16
HD = D // H
F = 1024
BT = 512
NT = BT // P
KD = D // P
KF = F // P
HB = S // BT
SCORE_SCALE = float(1.0 / np.sqrt(np.float32(H + 128 + 128)))
LN_EPS = 1e-5
RMS_EPS = 1e-8

TERMS = [(0, 0), (0, 1), (0, 2), (1, 0), (1, 1), (2, 0)]
ROWS = len(TERMS) * HD
GH = 4
NG = H // GH
KT = S // P
QT = S // P
LEAD = KT + 2

BANKS = 7
USES = (["ct"] * 2 + ["up"] * KF + ["qk"] * 8 + ["v"] * 2 + ["xT"] * 2 + ["yT"] * 2 + ["ss"] + ["down"] * 2 + [None])
assert len(USES) % BANKS == 0


def build_program(nc, x, wdq, bdq, wdkv, bdkv, wuq, buq, wqr, bqr, wkr, bkr, wuk, buk, wuv, buv, wo, bo,
                  wup, wdn, cos, sin, eye32, eye16, out):
    B = x.shape[0]
    parts_d = {n: nc.dram_tensor(f"{n}_parts", [B, 3, 2, P, S], BF16).ap() for n in "qk"}
    v_d = nc.dram_tensor("v_ones", [B, S, H, 2 * HD], F32).ap()
    gate_d = nc.dram_tensor("gate", [B, S, D], F32).ap()
    negmax_d = nc.dram_tensor("negmax", [2, GH * S], BF16).ap()
    den_d = nc.dram_tensor("den", [H, S], F32).ap()
    rden_d = nc.dram_tensor("rden", [H, S], F32).ap()

    with ExitStack() as ctx:
        def sem(name):
            return ctx.enter_context(nc.semaphore(name))

        with ExitStack() as part1:
            def sb(name, shape, dt=F32):
                return part1.enter_context(nc.sbuf_tensor(name, shape, dt))

            c = {
                "wdq": sb("wdq_s", [P, KD, P]), "wdkv": sb("wdkv_s", [P, KD, P]),
                "wuq": sb("wuq_s", [P, 2, P]), "wqr": sb("wqr_s", [P, 2, P]),
                "wkr": sb("wkr_s", [P, KD, 2, P]), "wuk": sb("wuk_s", [P, 2, P]),
                "wuv": sb("wuv_s", [P, D]), "buv": sb("buv_s", [P, D]),
                "bdq": sb("bdq_s", [P, 1]), "bdkv": sb("bdkv_s", [P, 1]),
                "buq": sb("buq_s", [P, 2]), "bqr": sb("bqr_s", [P, 2]),
                "bkr": sb("bkr_s", [P, 2]), "buk": sb("buk_s", [P, 2]),
                "cos": sb("cos_s", [P, S]), "sin": sb("sin_s", [P, S]),
                "eye32": sb("eye32_s", [P, P]), "eye16": sb("eye16_s", [P, P], F16),
                "wup": sb("wup_t", [P, KD, F], F16), "wdn": sb("wdn_t", [P, KF, D], F16),
                "ones": sb("ones_s", [P, P]), "halfs": sb("halfs", [P, NT]),
                "ln_eps": sb("ln_eps", [P, NT]), "rms_eps": sb("rms_eps", [P, NT]),
                "minus_halfs": sb("minus_halfs", [P, NT]), "minus_ones": sb("minus_ones", [P, NT]),
            }
            vx = sb("vx", [P, HB, NT, H, 2 * HD])
            sources = {
                "wdq": wdq.rearrange("(k p) m -> p k m", p=P), "wdkv": wdkv.rearrange("(k p) m -> p k m", p=P),
                "wuq": wuq, "wqr": wqr, "wkr": wkr.rearrange("(k p) e m -> p k e m", p=P), "wuk": wuk,
                "wuv": wuv, "buv": buv.partition_broadcast(P), "bdq": bdq, "bdkv": bdkv, "buq": buq,
                "bqr": bqr, "bkr": bkr, "buk": buk, "cos": cos, "sin": sin, "eye32": eye32, "eye16": eye16,
            }
            set_up(nc, sem, c, vx, sources, wup, wdn)
            project(nc, sem, sb, part1, B, c, vx, x, parts_d, v_d, gate_d)
        with ExitStack() as part2:
            attend(nc, sem, part2, B, x, wo, bo, parts_d, v_d, gate_d, negmax_d, den_d, rden_d, out)


def set_up(nc, sem, c, vx, sources, wup, wdn):
    with ExitStack() as ctx:
        def sb(name, shape, dt=F32):
            return ctx.enter_context(nc.sbuf_tensor(name, shape, dt))

        raw = {"wup": sb("wup_raw", [P, KD * F]), "wdn": sb("wdn_raw", [P, KF * D])}
        above = sb("above", [P, KD * F])
        below = sb("below", [P, KD * F])
        sums = sb("abs_sums", [P, 2])
        limit = sb("limit", [P, 2])
        minus_limit = sb("minus_limit", [P, 2])
        total = ctx.enter_context(nc.psum_tensor("abs_total", [P, 2], F32))
        weights_loaded, constants_loaded = sem("weights_loaded"), sem("constants_loaded")
        filled, summed, totalled = sem("filled"), sem("abs_summed"), sem("abs_totalled")
        limits, ternary = sem("limits"), sem("ternary")
        block = ctx.enter_context(nc.Block())

        @block.sync
        def _(sp):
            sp.dma_start(raw["wup"][:], wup.rearrange("(k p) f -> p k f", p=P)).then_inc(weights_loaded, 16)
            sp.dma_start(raw["wdn"][:], wdn.rearrange("(k p) d -> p k d", p=P)).then_inc(weights_loaded, 16)
            for name, source in sources.items():
                sp.dma_start(c[name][:], source).then_inc(constants_loaded, 16)
            sp.wait_ge(constants_loaded, 16 * len(sources))

        @block.gpsimd
        def _(pool):
            nc.gpsimd.memset(vx[:], 1.0)
            nc.gpsimd.memset(c["halfs"][:], 0.5)
            nc.gpsimd.memset(c["ln_eps"][:], LN_EPS)
            nc.gpsimd.memset(c["rms_eps"][:], RMS_EPS)
            nc.gpsimd.memset(c["minus_halfs"][:], -0.5)
            nc.gpsimd.memset(c["minus_ones"][:], -1.0)

        @block.tensor
        def _(pe):
            pe.wait_ge(filled, 1)
            pe.wait_ge(summed, 2)
            nc.tensor.matmul(total[:], c["ones"][:], sums[:], start=True, stop=True).then_inc(totalled, 1)

        @block.vector
        def _(dve):
            nc.vector.memset(c["ones"][:], 1.0).then_inc(filled, 1)
            dve.wait_ge(weights_loaded, 32)
            for i, name in enumerate(("wup", "wdn")):
                nc.vector.tensor_reduce(sums[:, i:i + 1], raw[name][:], AX.X, ALU.add,
                                        apply_absolute_value=True).then_inc(summed, 1)
            dve.wait_ge(totalled, 1)
            nc.vector.tensor_scalar(limit[:], total[:], 0.5 / (D * F), None, ALU.mult).then_inc(limits, 1)
            nc.vector.tensor_scalar(minus_limit[:], total[:], -0.5 / (D * F), None, ALU.mult).then_inc(limits, 1)
            dve.wait_ge(limits, 2)
            for i, name in enumerate(("wup", "wdn")):
                if i:
                    dve.wait_ge(ternary, 3)
                nc.vector.tensor_scalar(above[:], raw[name][:], limit[:, i:i + 1], None, ALU.is_gt).then_inc(ternary, 1)
                nc.vector.tensor_scalar(below[:], raw[name][:], minus_limit[:, i:i + 1], None,
                                        ALU.is_lt).then_inc(ternary, 1)
                dve.wait_ge(ternary, 3 * i + 2)
                flat = c[name][:].rearrange("p a b -> p (a b)")
                nc.vector.tensor_tensor(flat, above[:], below[:], ALU.subtract).then_inc(ternary, 1)


def project(nc, sem, sb, ctx, B, c, vx, x, parts_d, v_d, gate_d):
    x_s = sb("x_s", [P, 2, NT, D])
    stats = sb("stats", [P, NT, 6])
    mv = sb("mean_var", [P, NT, 2])
    ln = {k: sb(f"ln_{k}", [P, NT]) for k in ("ve", "rstd", "sd", "rms", "rmse", "r", "c2")}
    xn = sb("xn", [P, NT, D])
    y = sb("y", [P, NT, D])
    y_parts = sb("y_parts", [P, 2, NT, D], F16)
    xT = sb("xT", [P, KD, BT])
    yT = sb("yT", [P, KD, 2, BT], F16)
    ct = sb("ct", [P, 2, BT])
    rot = {n: sb(f"rot_{n}", [P, 4, BT]) for n in "qk"}
    rope = {n: sb(f"rope_{n}", [P, 2, BT]) for n in "qk"}
    full = {n: sb(f"full_{n}", [P, 2, BT]) for n in "qk"}
    rest = {n: sb(f"rest_{n}", [P, 2, BT]) for n in "qk"}
    part = {n: sb(f"part_{n}", [P, 3, 2, BT], BF16) for n in "qk"}
    h = sb("h", [P, KF, BT])
    h_parts = sb("h_parts", [P, 2, KF, BT], F16)
    sq = sb("sq", [P, 2, BT])
    sq_sum = sb("sq_sum", [P, BT])
    ms = {k: sb(f"ms_{k}", [P, NT]) for k in ("mean", "rms", "rmse", "r")}
    gate = sb("gate_s", [P, HB, NT, D])
    bank = [ctx.enter_context(nc.psum_tensor(f"bank{i}", [P, BT], F32)) for i in range(BANKS)]

    mm = {k: sem(f"{k}_in_psum") for k in ("ct", "up", "qk", "v", "xT", "yT", "ss", "down")}
    rd = {k: sem(f"{k}_read") for k in ("ct", "up", "qk", "v", "xT", "yT", "ss", "down")}
    READS = {"ct": 2, "up": KF, "qk": 8, "v": NT, "xT": 2, "yT": 2, "ss": 1, "down": NT}
    x_loaded = [sem(f"x_loaded{i}") for i in range(HB)]
    stats_complete = sem("stats_complete")
    stat_done, mv_done, ln_step = sem("stat_done"), sem("mv_done"), sem("ln_step")
    xn_ready, y_ready, yhi_ready, ylo_ready = sem("xn_ready"), sem("y_ready"), sem("yhi_ready"), sem("ylo_ready")
    hhi_ready, hlo_ready, sq_ready, sum_step = sem("hhi_ready"), sem("hlo_ready"), sem("sq_ready"), sem("sum_step")
    rope_ready, full_ready = sem("rope_ready"), sem("full_ready")
    p1_ready, rest_ready, p2_ready, p3_ready = sem("p1_ready"), sem("rest_ready"), sem("p2_ready"), sem("p3_ready")
    r_step = sem("r_step")
    parts_stored = {name: sem(f"parts_stored_{name}") for name in "qk"}
    v_stored = [sem(f"v_stored{i}") for i in range(HB)]
    gate_stored = [sem(f"gate_stored{i}") for i in range(HB)]
    LN_STEPS, R_STEPS = 7, 3

    def read_value(kind, i, n):
        per = READS[kind]
        last = {"v": 2 * i + 2, "down": 2 * i + 2}.get(kind, i + 1)
        return (n + 1 if kind in ("xT", "yT") else n) * per + last

    def wait_for_bank(pe, u, n, first):
        v = u - BANKS
        while USES[v % len(USES)] is None:
            v -= BANKS
        m = n
        if v < 0:
            v, m = v + len(USES), n - 1
            if first and USES[v] not in ("xT", "yT"):
                return
        kind = USES[v]
        pe.wait_ge(rd[kind], read_value(kind, v - USES.index(kind), m))

    block = ctx.enter_context(nc.Block())

    def each_block(eng, body):
        for hf in range(HB):
            body(0, hf, hf, hf == 0)
        with eng.Fori(1, B) as b:
            for hf in range(HB):
                body(b, b * HB + hf, hf, False)

    @block.sync
    def _(sp):
        def load_x(buf, b, hf):
            sp.dma_start(x_s[:, buf], x[b, hf * BT:(hf + 1) * BT, :].rearrange("(t p) d -> p t d", p=P)
                         ).then_inc(x_loaded[buf], 16)

        def body(b, n, hf, b_next, hf_next):
            sp.wait_ge(y_ready, n + 1)
            load_x(hf, b_next, hf_next)
            tokens = slice(hf * BT, (hf + 1) * BT)
            for name, k in (("q", 0), ("k", 1)):
                for i, ready in enumerate((p1_ready, p2_ready, p3_ready)):
                    sp.wait_ge(ready, 2 * n + k + 1)
                    sp.dma_start(parts_d[name][b, i].rearrange("e p t -> p e t")[:, :, tokens],
                                 part[name][:, i]).then_inc(parts_stored[name], 16)
            sp.wait_ge(rd["v"], NT * (n + 1))
            sp.dma_start(v_d[b, tokens].rearrange("(t p) h c -> p t (h c)", p=P),
                         vx[:, hf].rearrange("p t h c -> p t (h c)")).then_inc(v_stored[hf], 16)
            sp.wait_ge(rd["down"], NT * (n + 1))
            sp.dma_start(gate_d[b, tokens].rearrange("(t p) d -> p t d", p=P), gate[:, hf]).then_inc(gate_stored[hf], 16)

        load_x(0, 0, 0)
        load_x(1, 0, 1)
        with sp.Fori(0, B - 1) as b:
            for hf in range(HB):
                body(b, b * HB + hf, hf, b + 1, hf)
        for hf in range(HB):
            body(B - 1, (B - 1) * HB + hf, hf, B - 1, HB - 1)
        for hf in range(HB):
            sp.wait_ge(x_loaded[hf], 16 * (B + 1))
            sp.wait_ge(v_stored[hf], 16 * B)
            sp.wait_ge(gate_stored[hf], 16 * B)
        for name in "qk":
            sp.wait_ge(parts_stored[name], 16 * 3 * HB * B)

    @block.tensor
    def _(pe):
        def transposes(m, n, first):
            pe.wait_ge(xn_ready, m + 1)
            u = USES.index("xT")
            for k in range(KD):
                if n is not None:
                    wait_for_bank(pe, u + k, n, first)
                for t in range(NT):
                    last = nc.tensor.transpose(bank[(u + k) % BANKS][:, t * P:(t + 1) * P],
                                               xn[:, t, k * P:(k + 1) * P], c["eye32"][:])
                last.then_inc(mm["xT"], 1)
            pe.wait_ge(ylo_ready, m + 1)
            u = USES.index("yT")
            for k in range(KD):
                if n is not None:
                    wait_for_bank(pe, u + k, n, first)
                ps = bank[(u + k) % BANKS][:].bitcast(F16).rearrange("p (a t) -> p a t", a=2)
                for i in range(2):
                    for t in range(NT):
                        last = nc.tensor.transpose(ps[:, i, t * P:(t + 1) * P], y_parts[:, i, t, k * P:(k + 1) * P],
                                                   c["eye16"][:])
                last.then_inc(mm["yT"], 1)

        def body(b, n, hf, first):
            def product(kind, i, pairs, width=BT, at=0, done=True, wait=True):
                u = USES.index(kind) + i
                if wait:
                    wait_for_bank(pe, u, n, first)
                for j, (w, m) in enumerate(pairs):
                    last = nc.tensor.matmul(bank[u % BANKS][:, at:at + width], w, m, start=(j == 0),
                                            stop=(j == len(pairs) - 1))
                if done:
                    last.then_inc(mm[kind], 1)

            pe.wait_ge(rd["xT"], 2 * n + 2)
            for i, w in enumerate(("wdq", "wdkv")):
                product("ct", i, [(c[w][:, k], xT[:, k]) for k in range(KD)])
            pe.wait_ge(rd["yT"], 2 * n + 2)
            for f in range(KF):
                product("up", f, [(c["wup"][:, k, f * P:(f + 1) * P], yT[:, k, i]) for k in range(KD)
                                  for i in range(2)])
            pe.wait_ge(rd["ct"], 2 * n + 2)
            for e in range(2):
                product("qk", e, [(c["wqr"][:, e], ct[:, 0])])
            for e in range(2):
                product("qk", 2 + e, [(c["wkr"][:, k, e], xT[:, k]) for k in range(KD)])
            for e in range(2):
                product("qk", 4 + e, [(c["wuq"][:, e], ct[:, 0])])
            for e in range(2):
                product("qk", 6 + e, [(c["wuk"][:, e], ct[:, 1])])
            for t in range(NT):
                product("v", t // 2, [(ct[:, 1, t * P:(t + 1) * P], c["wuv"][:])], D, (t % 2) * D,
                        t % 2 == 1, t % 2 == 0)
            transposes(n + 1, n, first)
            pe.wait_ge(sum_step, (KF - 1) * (n + 1))
            u = USES.index("ss")
            wait_for_bank(pe, u, n, first)
            for t in range(NT):
                last = nc.tensor.matmul(bank[u % BANKS][:, t:t + 1], sq_sum[:, t * P:(t + 1) * P],
                                        c["ones"][:, 0:1], start=True, stop=True)
            last.then_inc(mm["ss"], 1)
            pe.wait_ge(hlo_ready, KF * (n + 1))
            for t in range(NT):
                product("down", t // 2, [(h_parts[:, i, f, t * P:(t + 1) * P], c["wdn"][:, f]) for f in range(KF)
                                         for i in range(2)], D, (t % 2) * D, t % 2 == 1, t % 2 == 0)

        transposes(0, None, True)
        each_block(pe, body)

    @block.scalar
    def _(act):
        def read_yT(m):
            u = USES.index("yT")
            for k in range(KD):
                act.wait_ge(mm["yT"], 2 * m + k + 1)
                nc.scalar.copy(yT[:, k].rearrange("p a t -> p (a t)"), bank[(u + k) % BANKS][:].bitcast(F16)
                               ).then_inc(rd["yT"], 1)

        def body(b, n, hf, first):
            for i, bias in enumerate(("bdq", "bdkv")):
                act.wait_ge(mm["ct"], 2 * n + i + 1)
                nc.scalar.activation(ct[:, i], bank[USES.index("ct") + i][:], ACT.Identity, bias=c[bias][:]
                                     ).then_inc(rd["ct"], 1)
            for f in range(KF):
                act.wait_ge(mm["up"], KF * n + f + 1)
                if not first:
                    act.wait_ge(hlo_ready, KF * n - KF + f + 1)
                nc.scalar.activation(h[:, f], bank[(USES.index("up") + f) % BANKS][:], ACT.Gelu
                                     ).then_inc(rd["up"], 1)
                act.wait_ge(rd["up"], KF * n + f + 1)
                if f == 0:
                    nc.scalar.activation(sq_sum[:], h[:, f], ACT.Square).then_inc(sq_ready, 1)
                else:
                    if f > 2:
                        act.wait_ge(sum_step, (KF - 1) * n + f - 2)
                    nc.scalar.activation(sq[:, f % 2], h[:, f], ACT.Square).then_inc(sq_ready, 1)
            read_yT(n + 1)
            act.wait_ge(r_step, R_STEPS * (n + 1))
            if not isinstance(b, int):
                act.wait_ge(gate_stored[hf], 16 * b)
            for t in range(NT):
                act.wait_ge(mm["down"], 2 * n + t // 2 + 1)
                u = USES.index("down") + t // 2
                nc.scalar.activation(gate[:, hf, t], bank[u % BANKS][:, (t % 2) * D:(t % 2 + 1) * D], ACT.Silu,
                                     scale=ms["r"][:, t:t + 1]).then_inc(rd["down"], 1)

        read_yT(0)
        each_block(act, body)

    @block.vector
    def _(dve):
        def statistics(m, buf, loads):
            dve.wait_ge(x_loaded[buf], 16 * loads)
            for t in range(NT):
                nc.vector.bn_stats(stats[:, t], x_s[:, buf, t]).then_inc(stat_done, 1)
            dve.wait_ge(stat_done, NT * m + NT)
            dve.sem_inc(stats_complete)
            for t in range(NT):
                nc.vector.bn_aggr(mv[:, t], stats[:, t]).then_inc(mv_done, 1)

        def normalise(m, buf, first):
            dve.wait_ge(ln_step, LN_STEPS * m + LN_STEPS)
            if not first:
                dve.wait_ge(mm["xT"], 2 * m)
            for t in range(NT):
                last = nc.vector.tensor_scalar(xn[:, t], x_s[:, buf, t], mv[:, t, 0:1], ln["rstd"][:, t:t + 1],
                                               ALU.subtract, ALU.mult)
            last.then_inc(xn_ready, 1)
            if not first:
                dve.wait_ge(ylo_ready, m)
            for t in range(NT):
                last = nc.vector.tensor_scalar(y[:, t], x_s[:, buf, t], mv[:, t, 0:1], ln["c2"][:, t:t + 1],
                                               ALU.subtract, ALU.mult)
            last.then_inc(y_ready, 1)
            dve.wait_ge(y_ready, m + 1)
            if not first:
                dve.wait_ge(mm["yT"], 2 * m)
            nc.vector.tensor_copy(y_parts[:, 0], y[:]).then_inc(yhi_ready, 1)

        def read_xT(m):
            u = USES.index("xT")
            for k in range(KD):
                dve.wait_ge(mm["xT"], 2 * m + k + 1)
                nc.vector.tensor_copy(xT[:, k], bank[(u + k) % BANKS][:]).then_inc(rd["xT"], 1)

        def body(b, n, hf, first):
            statistics(n + 1, (hf + 1) % 2, b + hf + 1)
            for f in range(KF):
                dve.wait_ge(rd["up"], KF * n + f + 1)
                nc.vector.tensor_copy(h_parts[:, 0, f], h[:, f]).then_inc(hhi_ready, 1)
                dve.wait_ge(hhi_ready, KF * n + f + 1)
                nc.vector.tensor_tensor(h_parts[:, 1, f], h[:, f], h_parts[:, 0, f], ALU.subtract
                                        ).then_inc(hlo_ready, 1)
            normalise(n + 1, (hf + 1) % 2, False)
            tokens = slice(hf * BT, (hf + 1) * BT)
            u = USES.index("qk")
            for j, (name, bias) in enumerate((("q", "bqr"), ("k", "bkr"))):
                if not first:
                    dve.wait_ge(rope_ready, 4 * n - 2 + 2 * j)
                for e in range(2):
                    i = 2 * j + e
                    dve.wait_ge(mm["qk"], 8 * n + i + 1)
                    ps = bank[(u + i) % BANKS][:]
                    b_ = c[bias][:, e:e + 1]
                    nc.vector.scalar_tensor_tensor(rot[name][:, 2 * e], ps, b_, c["cos" if e == 0 else "sin"][:, tokens],
                                                   ALU.add, ALU.mult)
                    nc.vector.scalar_tensor_tensor(rot[name][:, 2 * e + 1], ps, b_,
                                                   c["sin" if e == 0 else "cos"][:, tokens], ALU.add, ALU.mult
                                                   ).then_inc(rd["qk"], 1)
            for j, (name, bias) in enumerate((("q", "buq"), ("k", "buk"))):
                if not first:
                    dve.wait_ge(rest_ready, 2 * n - 1 + j)
                for e in range(2):
                    i = 4 + 2 * j + e
                    dve.wait_ge(mm["qk"], 8 * n + i + 1)
                    dve.wait_ge(rope_ready, 4 * n + 2 * j + e + 1)
                    nc.vector.scalar_tensor_tensor(full[name][:, e], bank[(u + i) % BANKS][:], c[bias][:, e:e + 1],
                                                   rope[name][:, e], ALU.add, ALU.add).then_inc(rd["qk"], 1)
                dve.wait_ge(rd["qk"], 8 * n + 6 + 2 * j)
                if not first:
                    dve.wait_ge(parts_stored[name], 48 * n)
                nc.vector.tensor_copy(part[name][:, 0], full[name][:]).then_inc(p1_ready, 1)
            for t in range(NT):
                if t == 0 and not isinstance(b, int):
                    dve.wait_ge(v_stored[hf], 16 * b)
                dve.wait_ge(mm["v"], 2 * n + t // 2 + 1)
                ps = bank[(USES.index("v") + t // 2) % BANKS][:, (t % 2) * D:(t % 2 + 1) * D]
                nc.vector.tensor_tensor(vx[:, hf, t, :, 0:HD], ps.rearrange("p (h c) -> p h c", c=HD),
                                        c["buv"][:].rearrange("p (h c) -> p h c", c=HD), ALU.add
                                        ).then_inc(rd["v"], 1)
            for j, name in enumerate("qk"):
                dve.wait_ge(rest_ready, 2 * n + j + 1)
                nc.vector.tensor_copy(part[name][:, 1], rest[name][:]).then_inc(p2_ready, 1)
            read_xT(n + 1)
            dve.wait_ge(mm["ss"], n + 1)
            nc.vector.tensor_scalar(ms["mean"][:], bank[USES.index("ss") % BANKS][:, 0:NT], 1.0 / F, None, ALU.mult
                                    ).then_inc(rd["ss"], 1)

        statistics(0, 0, 1)
        normalise(0, 0, True)
        read_xT(0)
        each_block(dve, body)

    @block.gpsimd
    def _(pool):
        def factors(m):
            g, at = nc.gpsimd, LN_STEPS * m
            pool.wait_ge(mv_done, NT * m + NT)
            var = mv[:, :, 1]
            g.tensor_tensor(ln["ve"][:], var, c["ln_eps"][:], ALU.add).then_inc(ln_step, 1)
            g.tensor_tensor(ln["sd"][:], var, c["halfs"][:], ALU.pow).then_inc(ln_step, 1)
            pool.wait_ge(ln_step, at + 1)
            g.tensor_tensor(ln["rstd"][:], ln["ve"][:], c["minus_halfs"][:], ALU.pow).then_inc(ln_step, 1)
            pool.wait_ge(ln_step, at + 3)
            g.tensor_tensor(ln["rms"][:], ln["sd"][:], ln["rstd"][:], ALU.mult).then_inc(ln_step, 1)
            pool.wait_ge(ln_step, at + 4)
            g.tensor_tensor(ln["rmse"][:], ln["rms"][:], c["rms_eps"][:], ALU.add).then_inc(ln_step, 1)
            pool.wait_ge(ln_step, at + 5)
            g.tensor_tensor(ln["r"][:], ln["rmse"][:], c["minus_ones"][:], ALU.pow).then_inc(ln_step, 1)
            pool.wait_ge(ln_step, at + 6)
            g.tensor_tensor(ln["c2"][:], ln["rstd"][:], ln["r"][:], ALU.mult).then_inc(ln_step, 1)

        def lower_part(m, first):
            pool.wait_ge(yhi_ready, m + 1)
            if not first:
                pool.wait_ge(mm["yT"], 2 * m)
            nc.gpsimd.tensor_tensor(y_parts[:, 1], y[:], y_parts[:, 0], ALU.subtract).then_inc(ylo_ready, 1)

        def body(b, n, hf, first):
            factors(n + 1)
            for f in range(1, KF):
                pool.wait_ge(sq_ready, KF * n + f + 1)
                if f > 1:
                    pool.wait_ge(sum_step, (KF - 1) * n + f - 1)
                nc.gpsimd.tensor_tensor(sq_sum[:], sq_sum[:], sq[:, f % 2], ALU.add).then_inc(sum_step, 1)
            lower_part(n + 1, False)
            for j, name in enumerate("qk"):
                r = rot[name]
                pool.wait_ge(rd["qk"], 8 * n + 2 * j + 2)
                if not first:
                    pool.wait_ge(p1_ready, 2 * n)
                nc.gpsimd.tensor_tensor(rope[name][:, 0], r[:, 0], r[:, 2], ALU.subtract).then_inc(rope_ready, 1)
                nc.gpsimd.tensor_tensor(rope[name][:, 1], r[:, 3], r[:, 1], ALU.add).then_inc(rope_ready, 1)
            for j, name in enumerate("qk"):
                pool.wait_ge(p1_ready, 2 * n + j + 1)
                if not first:
                    pool.wait_ge(p3_ready, 2 * n - 1 + j)
                nc.gpsimd.tensor_tensor(rest[name][:], full[name][:], part[name][:, 0], ALU.subtract
                                        ).then_inc(rest_ready, 1)
            for j, name in enumerate("qk"):
                pool.wait_ge(p2_ready, 2 * n + j + 1)
                nc.gpsimd.tensor_tensor(part[name][:, 2], rest[name][:], part[name][:, 1], ALU.subtract
                                        ).then_inc(p3_ready, 1)
            at = R_STEPS * n
            pool.wait_ge(rd["ss"], n + 1)
            nc.gpsimd.tensor_tensor(ms["rms"][:], ms["mean"][:], c["halfs"][:], ALU.pow).then_inc(r_step, 1)
            pool.wait_ge(r_step, at + 1)
            nc.gpsimd.tensor_tensor(ms["rmse"][:], ms["rms"][:], c["rms_eps"][:], ALU.add).then_inc(r_step, 1)
            pool.wait_ge(r_step, at + 2)
            if not first:
                pool.wait_ge(rd["down"], NT * n)
            nc.gpsimd.tensor_tensor(ms["r"][:], ms["rmse"][:], c["minus_ones"][:], ALU.pow).then_inc(r_step, 1)

        factors(0)
        lower_part(0, True)
        each_block(pool, body)


def attend(nc, sem, ctx, B, x, wo, bo, parts_d, v_d, gate_d, negmax_d, den_d, rden_d, out):
    def sb(name, shape, dt=F32):
        return ctx.enter_context(nc.sbuf_tensor(name, shape, dt))

    stack = {n: sb(f"stack_{n}", [ROWS + 1, NG, GH, S], BF16) for n in "qk"}
    v_s = sb("v_s", [P, NG, KT, GH, 2 * HD])
    probs = sb("probs", [P, 2, GH, S])
    maxima = sb("maxima", [P, 2, GH * QT, 2])
    negmax = sb("negmax_s", [P, 2, GH * QT], BF16)
    negmax_t = sb("negmax_t", [P, 2, GH * QT], BF16)
    raw = sb("raw", [P, 2, S])
    o = sb("o", [P, KD, S])
    den = sb("den_s", [P, P])
    rden = sb("rden_s", [P, P])
    rden_b = sb("rden_b", [P, KD, S])
    wo_s = sb("wo_s", [P, KD, D])
    bo_s = sb("bo_s", [P, D])
    res = sb("res", [P, 2, NT, D])
    x_r = sb("x_r", [P, 2, NT, D])
    gate_r = sb("gate_r", [P, 2, NT, D])
    scores = ctx.enter_context(nc.psum_tensor("scores", [P, 2, S], F32))
    for_max = ctx.enter_context(nc.psum_tensor("for_max", [P, 2, BT], F32))
    sums = ctx.enter_context(nc.psum_tensor("sums", [P, S], F32))

    loaded2, ones_set = sem("wo_loaded"), sem("ones_set")
    stack_loaded = [sem(f"stack_loaded{g}") for g in range(NG)]
    st_full, exp_done, pv_done, evacuated = sem("st_full"), sem("exp_done"), sem("pv_done"), sem("evacuated")
    max_full, max_free = sem("max_full"), sem("max_free")
    negmax_ready, negmax_turned = sem("negmax_ready"), sem("negmax_turned")
    negmax_out, shift_loaded = sem("negmax_out"), sem("shift_loaded")
    heads_placed = [sem(f"heads_placed{i}") for i in range(2)]
    den_loaded = sem("den_loaded")
    rden_ready, rden_out, rden_loaded = sem("rden_ready"), sem("rden_out"), sem("rden_loaded")
    o_ready, y_full, y_read, res_step = sem("o_ready"), sem("y_full"), sem("y_read"), sem("res_step")
    sync_passed = sem("sync_passed")
    xg_loaded, out_stored = sem("xg_loaded"), sem("out_stored")
    STACK_DMAS = 2 * 2 * len(TERMS) + 1
    UNIT = 8

    block = ctx.enter_context(nc.Block())

    def ahead(g, s):
        u = g * KT + s + LEAD
        return u // (NG * KT), (u // KT) % NG, u % KT

    @block.sync
    def _(sp):
        def wait(what, value):
            sp.wait_ge(what, value)
            sp.sem_inc(sync_passed)

        def load_group(b, g):
            for k, name in enumerate("qk"):
                for t, pair in enumerate(TERMS):
                    for e in range(2):
                        r = t * HD + e * HD // 2
                        rows = parts_d[name][b, pair[k], e, g * GH * HD // 2:(g + 1) * GH * HD // 2, :]
                        sp.dma_start(stack[name][r:r + HD // 2, g], rows.rearrange("(j i) t -> i j t", i=HD // 2)
                                     ).then_inc(stack_loaded[g], 16)
            sp.dma_start(v_s[:, g], v_d[b, :, g * GH:(g + 1) * GH, :].rearrange("(k p) j c -> p k j c", p=P)
                         ).then_inc(stack_loaded[g], 16)

        def shift_rows(b, g):
            G, par = b * NG + g, g % 2
            wait(negmax_turned, G + 1)
            for q in range(4):
                sp.dma_start(negmax_d[par].rearrange("(c q r) -> q c r", q=4, r=32)[q],
                             negmax_t[32 * q:32 * q + 32, par, :]).then_inc(negmax_out, 16)
            wait(negmax_out, G * 64 + 64)
            sp.dma_start(stack["q"][ROWS:ROWS + 1, g].rearrange("p j t -> p (j t)"), negmax_d[par:par + 1, :]
                         ).then_inc(shift_loaded, 16)

        def place_heads(b, g):
            wait(evacuated, b * NG + g + 1)
            for j in range(GH):
                head = g * GH + j
                at = (head * HD) % P
                sp.dma_start(o[at:at + HD, head * HD // P], raw[32 * j:32 * j + HD, g % 2]
                             ).then_inc(heads_placed[g % 2], 16)
            sp.dma_start(den_d[g * GH:(g + 1) * GH, :], raw[HD:P:32, g % 2]).then_inc(heads_placed[g % 2], 16)

        def spread_denominators(b):
            for placed in heads_placed:
                wait(placed, 40 * NG * b + 40 * NG)
            sp.dma_start(den[:], den_d.rearrange("h (a c) -> (h a) c", c=P)).then_inc(den_loaded, 16)
            wait(rden_ready, b + 1)
            sp.dma_start(rden_d.rearrange("h (a c) -> (h a) c", c=P), rden[:]).then_inc(rden_out, 16)
            wait(rden_out, 16 * b + 16)
            for i in range(P // HD):
                sp.dma_start(rden_b[i * HD:(i + 1) * HD], rden_d.rearrange("(k h) t -> h k t", k=KD)[i]
                             .partition_broadcast(HD)).then_inc(rden_loaded, 16)

        def load_residual(b):
            for k in range(2):
                tokens = slice(k * BT, (k + 1) * BT)
                sp.dma_start(x_r[:, k], x[b, tokens].rearrange("(t p) d -> p t d", p=P)).then_inc(xg_loaded, 16)
                sp.dma_start(gate_r[:, k], gate_d[b, tokens].rearrange("(t p) d -> p t d", p=P)
                             ).then_inc(xg_loaded, 16)

        def T(b, g, last):
            first = isinstance(b, int) and b == 0 and g == 0
            G = b * NG + g
            if not last:
                if not first:
                    wait(st_full, GH * KT * G)
                    wait(pv_done, KT * G)
                load_group(*((b, 3) if g == 0 else (b + 1, g - 1)))
            elif first:
                load_group(b, 3)
            if not first:
                place_heads(*((b, g - 1) if g else (b - 1, NG - 1)))
            if g == 0 and not first:
                spread_denominators(b - 1)
            if g == NG - 1:
                load_residual(b)
            if g < NG - 1:
                shift_rows(b, g + 1)
            elif not last:
                shift_rows(b + 1, 0)

        def O(b):
            for k in range(2):
                wait(res_step, 6 * b + 3 * k + 3)
                sp.dma_start(out[b, k * BT:(k + 1) * BT].rearrange("(t p) d -> p t d", p=P), res[:, k]
                             ).then_inc(out_stored, 16)

        def last_O(b):
            place_heads(b, NG - 1)
            spread_denominators(b)
            O(b)

        sp.dma_start(wo_s[:], wo.rearrange("(k p) n -> p k n", p=P)).then_inc(loaded2, 16)
        sp.dma_start(bo_s[:], bo.partition_broadcast(P)).then_inc(loaded2, 16)
        for g in range(3):
            load_group(0, g)
        shift_rows(0, 0)
        T(0, 0, B == 1)
        if B > 1:
            with sp.Fori(0, B - 1) as b:
                for g in range(1, NG):
                    T(b, g, False)
                T(b + 1, 0, False)
                O(b)
        for g in range(1, NG):
            T(B - 1, g, True)
        last_O(B - 1)
        wait(out_stored, 32 * B)
        for g in range(NG):
            wait(stack_loaded[g], 16 * STACK_DMAS * B)

    @block.tensor
    def _(pe):
        def maxima_products(b, g, u):
            if u == 0:
                pe.wait_ge(stack_loaded[g], b * 16 * STACK_DMAS + 16 * STACK_DMAS)
            j = u // 2
            made = []
            for i in range(UNIT):
                made.append((j, 4 * (u % 2) + i // 2, i % 2, i))
            return made

        def one_maxima_product(b, g, u, item):
            j, qt, half, i = item
            index = (b * NG + g) * KT * UNIT + u * UNIT + i
            if not (isinstance(index, int) and index < 2):
                pe.wait_ge(max_free, index - 1)
            nc.tensor.matmul(for_max[:, half], stack["q"][0:ROWS, g, j, qt * P:(qt + 1) * P],
                             stack["k"][0:ROWS, g, j, half * BT:(half + 1) * BT], start=True, stop=True
                             ).then_inc(max_full, 1)

        def pv(b, g, s, half):
            n = (b * NG + g) * KT + s
            if half == 0:
                pe.wait_ge(exp_done, n * GH + GH)
                if s == 0 and not (isinstance(n, int) and n == 0):
                    pe.wait_ge(evacuated, b * NG + g)
            for j in range(GH):
                last = nc.tensor.matmul(sums[32 * j:32 * j + 32, half * BT:(half + 1) * BT], v_s[:, g, s, j],
                                        probs[:, s % 2, j, half * BT:(half + 1) * BT], start=(s == 0),
                                        stop=(s == KT - 1))
            if half == 1:
                last.then_inc(pv_done, 1)

        def T(b, g, last):
            G = b * NG + g
            first = isinstance(b, int) and b == 0 and g == 0
            pe.wait_ge(shift_loaded, 16 * G + 16)
            for s in range(KT):
                db, mg, u = ahead(g, s)
                items = [] if last and db else maxima_products(b + db, mg, u)
                for j in range(GH):
                    e = G * KT * GH + s * GH + j
                    if not (first and s == 0 and j < 2):
                        pe.wait_ge(exp_done, e - 1)
                    for half in range(2):
                        mm = nc.tensor.matmul(scores[:, j % 2, half * BT:(half + 1) * BT],
                                              stack["k"][:, g, j, s * P:(s + 1) * P],
                                              stack["q"][:, g, j, half * BT:(half + 1) * BT], start=True, stop=True)
                    mm.then_inc(st_full, 1)
                    for item in items[2 * j:2 * j + 2]:
                        one_maxima_product(b + db, mg, u, item)
                    if j % 2 and not (first and s == 0):
                        before = (b, g, s - 1) if s else ((b, g - 1, KT - 1) if g else (b - 1, NG - 1, KT - 1))
                        pv(*before, j // 2)

        def O(b, tail=False):
            if tail:
                pv(b, NG - 1, KT - 1, 0)
                pv(b, NG - 1, KT - 1, 1)
                pe.wait_ge(exp_done, GH * KT * NG * B)
            else:
                pe.wait_ge(exp_done, (b * NG + NG + 1) * KT * GH)
            pe.wait_ge(o_ready, 2 * b + 2)
            for k in range(2):
                for t in range(NT):
                    for i in range(KD):
                        mm = nc.tensor.matmul(scores[:, k, t * D:(t + 1) * D],
                                              o[:, i, (k * NT + t) * P:(k * NT + t + 1) * P], wo_s[:, i],
                                              start=(i == 0), stop=(i == KD - 1))
                mm.then_inc(y_full, 1)
            pe.wait_ge(y_read, 2 * b + 2)

        pe.wait_ge(loaded2, 32)
        pe.wait_ge(ones_set, 1)
        for n in range(LEAD):
            g, u = n // KT, n % KT
            for item in maxima_products(0, g, u):
                one_maxima_product(0, g, u, item)
        T(0, 0, B == 1)
        if B > 1:
            with pe.Fori(0, B - 1) as b:
                for g in range(1, NG):
                    T(b, g, False)
                T(b + 1, 0, False)
                O(b)
        for g in range(1, NG):
            T(B - 1, g, True)
        O(B - 1, True)

    @block.scalar
    def _(act):
        def evacuate(b, g):
            act.wait_ge(pv_done, (b * NG + g) * KT + KT)
            if g >= 2:
                act.wait_ge(heads_placed[g % 2], 40 * NG * b + 80)
            nc.scalar.copy(raw[:, g % 2], sums[:]).then_inc(evacuated, 1)

        def T(b, g, last):
            G = b * NG + g
            first = isinstance(b, int) and b == 0 and g == 0
            for s in range(KT):
                n = G * KT + s
                if s == 1 and not first:
                    evacuate(*((b, g - 1) if g else (b - 1, NG - 1)))
                for j in range(GH):
                    e = n * GH + j
                    act.wait_ge(st_full, e + 1)
                    if j == 0 and not (first and s < 2):
                        act.wait_ge(pv_done, n - 1)
                    nc.scalar.activation(probs[:, s % 2, j], scores[:, j % 2], ACT.Exp, scale=SCORE_SCALE
                                         ).then_inc(exp_done, 1)

        def O(b, tail=False):
            if tail:
                evacuate(b, NG - 1)
            for k in range(2):
                act.wait_ge(y_full, 2 * b + k + 1)
                nc.scalar.copy(res[:, k].rearrange("p t d -> p (t d)"), scores[:, k]).then_inc(y_read, 1)

        T(0, 0, B == 1)
        if B > 1:
            with act.Fori(0, B - 1) as b:
                for g in range(1, NG):
                    T(b, g, False)
                T(b + 1, 0, False)
                O(b)
        for g in range(1, NG):
            T(B - 1, g, True)
        O(B - 1, True)

    @block.vector
    def _(dve):
        def reduce_unit(b, g, u):
            G, par = b * NG + g, g % 2
            for i in range(UNIT):
                index = G * KT * UNIT + u * UNIT + i
                dve.wait_ge(max_full, index + 1)
                nc.vector.tensor_reduce(maxima[:, par, u * UNIT // 2 + i // 2, i % 2:i % 2 + 1], for_max[:, i % 2],
                                        AX.X, ALU.max).then_inc(max_free, 1)
            if u == KT - 1:
                dve.wait_ge(max_free, G * KT * UNIT + KT * UNIT)
                nc.vector.tensor_reduce(negmax[:, par], maxima[:, par], AX.X, ALU.max, negate=True
                                        ).then_inc(negmax_ready, 1)
                dve.wait_ge(negmax_ready, G + 1)
                if not (isinstance(b, int) and b == 0 and g < 2):
                    dve.wait_ge(negmax_out, 64 * G - 64)
                nc.vector.transpose(negmax_t[:, par], negmax[:, par]).then_inc(negmax_turned, 1)

        def invert(b):
            dve.wait_ge(den_loaded, 16 * b + 16)
            nc.vector.reciprocal(rden[:], den[:]).then_inc(rden_ready, 1)

        def T(b, g, last):
            first = isinstance(b, int) and b == 0 and g == 0
            for s in range(KT):
                db, mg, u = ahead(g, s)
                if not (last and db):
                    reduce_unit(b + db, mg, u)
                if g == 0 and s == 5 and not first:
                    invert(b - 1)

        nc.vector.memset(stack["k"][ROWS:ROWS + 1], 1.0).then_inc(ones_set, 1)
        for n in range(LEAD):
            reduce_unit(0, n // KT, n % KT)
        T(0, 0, B == 1)
        if B > 1:
            with dve.Fori(0, B - 1) as b:
                for g in range(1, NG):
                    T(b, g, False)
                T(b + 1, 0, False)
        for g in range(1, NG):
            T(B - 1, g, True)
        invert(B - 1)

    @block.gpsimd
    def _(pool):
        def O(b):
            pool.wait_ge(rden_loaded, 16 * (P // HD) * b + 16 * (P // HD))
            for i in range(KD):
                nc.gpsimd.tensor_tensor(o[:, i], o[:, i], rden_b[:, i], ALU.mult).then_inc(o_ready, 1)
            pool.wait_ge(xg_loaded, 64 * b + 64)
            for k in range(2):
                r = res[:, k]
                pool.wait_ge(y_read, 2 * b + k + 1)
                nc.gpsimd.tensor_tensor(r, r, bo_s[:].unsqueeze(1).to_broadcast([P, NT, D]), ALU.add
                                        ).then_inc(res_step, 1)
                pool.wait_ge(res_step, 6 * b + 3 * k + 1)
                nc.gpsimd.tensor_tensor(r, r, gate_r[:, k], ALU.mult).then_inc(res_step, 1)
                pool.wait_ge(res_step, 6 * b + 3 * k + 2)
                nc.gpsimd.tensor_tensor(r, r, x_r[:, k], ALU.add).then_inc(res_step, 1)
            pool.wait_ge(out_stored, 32 * b + 32)

        pool.wait_ge(loaded2, 32)
        if B > 1:
            with pool.Fori(0, B - 1) as b:
                O(b)
        O(B - 1)


_NAMES = ["x", "wdq", "bdq", "wdkv", "bdkv", "wuq", "buq", "wqr", "bqr", "wkr", "bkr", "wuk", "buk", "wuv", "buv",
          "wo", "bo", "wup", "wdn", "cos", "sin", "eye32", "eye16"]


def lay_out(i):
    def eo(w):
        return np.ascontiguousarray(w.reshape(w.shape[0], D // 2, 2).transpose(0, 2, 1))

    def col(v):
        return np.ascontiguousarray(v.reshape(-1, 1))

    def pair(v):
        return np.ascontiguousarray(v.reshape(D // 2, 2))

    a = {k: np.asarray(v) for k, v in i.items()}
    f = lambda name: a["L0_attn_" + name]
    position = np.arange(S, dtype=np.float32)[:, None]
    ids = np.arange(D // 2, dtype=np.float32)
    theta = (np.float32(10000.0) ** (np.float32(-2.0) * ids)) / np.float32(D // 2)
    angle = (position * theta[None, :]).astype(np.float32)
    return {
        "x": f("x"), "wdq": f("Wd_q_w"), "bdq": col(f("Wd_q_b")), "wdkv": f("Wd_kv_w"), "bdkv": col(f("Wd_kv_b")),
        "wuq": eo(f("Wu_q_w")), "buq": pair(f("Wu_q_b")), "wqr": eo(f("Wq_r_w")), "bqr": pair(f("Wq_r_b")),
        "wkr": eo(f("Wk_r_w")), "bkr": pair(f("Wk_r_b")), "wuk": eo(f("Wu_k_w")), "buk": pair(f("Wu_k_b")),
        "wuv": f("Wu_v_w"), "buv": f("Wu_v_b"), "wo": f("Wo_w"), "bo": f("Wo_b"),
        "wup": np.ascontiguousarray(a["L0_ffn_w_up"].T), "wdn": np.ascontiguousarray(a["L0_ffn_w_down"].T),
        "cos": np.ascontiguousarray(np.cos(angle).T), "sin": np.ascontiguousarray(np.sin(angle).T),
        "eye32": np.eye(P, dtype=np.float32), "eye16": np.eye(P, dtype=np.float16),
    }


def kernel(**inputs):
    import concourse.bacc as bacc
    from concourse.bass_utils import run_bass_kernel_spmd as run

    nc = bacc.Bacc("TRN2", target_bir_lowering=False, num_devices=1)
    laid = lay_out(inputs)
    arrays = {f"in_{n}": np.ascontiguousarray(laid[n]) for n in _NAMES}
    args = [nc.dram_tensor(f"in_{n}", arrays[f"in_{n}"].shape, mybir.dt.from_np(arrays[f"in_{n}"].dtype),
                           kind="ExternalInput").ap() for n in _NAMES]
    out = nc.dram_tensor("out_0", laid["x"].shape, F32, kind="ExternalOutput").ap()
    build_program(nc, *args, out)
    r = run(nc, [arrays], core_ids=[0])
    return r.results[0]["out_0"]
```

```python
from contextlib import ExitStack

import numpy as np

import concourse.bass as bass
from concourse import mybir

F32 = mybir.dt.float32
F16 = mybir.dt.float16
BF16 = mybir.dt.bfloat16
ALU = mybir.AluOpType
ACT = mybir.ActivationFunctionType
AX = mybir.AxisListType

P = 128
S = 1024
D = 256
H = 16
HD = D // H
F = 1024
BT = 512
NT = BT // P
KD = D // P
KF = F // P
HB = S // BT
SCORE_SCALE = float(1.0 / np.sqrt(np.float32(H + 128 + 128)))
LN_EPS = 1e-5
RMS_EPS = 1e-8

TERMS = [(0, 0), (0, 1), (0, 2), (1, 0), (1, 1), (2, 0)]
ROWS = len(TERMS) * HD
GH = 4
NG = H // GH
SAMPLE = 16
HEADROOM = 40.0
DEN_LIMIT = 1e25
KT = S // P
QT = S // P
LEAD = KT + 2

BANKS = 7
USES = (["ct"] * 2 + ["up"] * KF + ["qk"] * 8 + ["ss"] + ["down"] * 2 + ["xT"] * 2 + ["yT"] * 2 + ["v"] * 2 + [None])
assert len(USES) % BANKS == 0


def build_program(nc, x, wdq, bdq, wdkv, bdkv, wuq, buq, wqr, bqr, wkr, bkr, wuk, buk, wuv, buv, wo, bo,
                  wup, wdn, cos, sin, eye32, eye16, out):
    B = x.shape[0]
    parts_d = {n: nc.dram_tensor(f"{n}_parts", [B, 3, 2, P, S], BF16).ap() for n in "qk"}
    v_d = nc.dram_tensor("v_ones", [B, S, H, 2 * HD], F32).ap()
    gate_d = nc.dram_tensor("gate", [B, S, D], F32).ap()
    negmax_d = nc.dram_tensor("negmax", [2, GH * S], BF16).ap()
    den_d = nc.dram_tensor("den", [H, S], F32).ap()
    rden_d = nc.dram_tensor("rden", [H, S], F32).ap()

    with ExitStack() as ctx:
        def sem(name):
            return ctx.enter_context(nc.semaphore(name))

        with ExitStack() as part1:
            def sb(name, shape, dt=F32):
                return part1.enter_context(nc.sbuf_tensor(name, shape, dt))

            c = {
                "wdq": sb("wdq_s", [P, KD, P]), "wdkv": sb("wdkv_s", [P, KD, P]),
                "wuq": sb("wuq_s", [P, 2, P]), "wqr": sb("wqr_s", [P, 2, P]),
                "wkr": sb("wkr_s", [P, KD, 2, P]), "wuk": sb("wuk_s", [P, 2, P]),
                "wuv": sb("wuv_s", [P, D]), "buv": sb("buv_s", [P, D]),
                "bdq": sb("bdq_s", [P, 1]), "bdkv": sb("bdkv_s", [P, 1]),
                "buq": sb("buq_s", [P, 2]), "bqr": sb("bqr_s", [P, 2]),
                "bkr": sb("bkr_s", [P, 2]), "buk": sb("buk_s", [P, 2]),
                "cos": sb("cos_s", [P, S]), "sin": sb("sin_s", [P, S]),
                "eye32": sb("eye32_s", [P, P]), "eye16": sb("eye16_s", [P, P], F16),
                "wup": sb("wup_t", [P, KD, F], F16), "wdn": sb("wdn_t", [P, KF, D], F16),
                "ones": sb("ones_s", [P, P]), "halfs": sb("halfs", [P, 2, NT]),
            }
            vx = sb("vx", [P, HB, NT, H, 2 * HD])
            sources = {
                "wdq": wdq.rearrange("(k p) m -> p k m", p=P), "wdkv": wdkv.rearrange("(k p) m -> p k m", p=P),
                "wuq": wuq, "wqr": wqr, "wkr": wkr.rearrange("(k p) e m -> p k e m", p=P), "wuk": wuk,
                "wuv": wuv, "buv": buv.partition_broadcast(P), "bdq": bdq, "bdkv": bdkv, "buq": buq,
                "bqr": bqr, "bkr": bkr, "buk": buk, "cos": cos, "sin": sin, "eye32": eye32, "eye16": eye16,
            }
            set_up(nc, sem, c, vx, sources, wup, wdn)
            project(nc, sem, sb, part1, B, c, vx, x, parts_d, v_d, gate_d)
        repeat = ctx.enter_context(nc.sbuf_tensor("repeat", [P, 1], mybir.dt.int32))
        for exact in (False, True):
            with ExitStack() as part2:
                attend(nc, sem, part2, exact, repeat, B, x, wo, bo, parts_d, v_d, gate_d, negmax_d, den_d, rden_d,
                       out)


def set_up(nc, sem, c, vx, sources, wup, wdn):
    with ExitStack() as ctx:
        def sb(name, shape, dt=F32):
            return ctx.enter_context(nc.sbuf_tensor(name, shape, dt))

        raw = {"wup": sb("wup_raw", [P, KD * F]), "wdn": sb("wdn_raw", [P, KF * D])}
        above = sb("above", [P, KD * F])
        below = sb("below", [P, KD * F])
        sums = sb("abs_sums", [P, 2])
        limit = sb("limit", [P, 2])
        minus_limit = sb("minus_limit", [P, 2])
        total = ctx.enter_context(nc.psum_tensor("abs_total", [P, 2], F32))
        weights_loaded, constants_loaded = sem("weights_loaded"), sem("constants_loaded")
        filled, summed, totalled = sem("filled"), sem("abs_summed"), sem("abs_totalled")
        limits, ternary = sem("limits"), sem("ternary")
        block = ctx.enter_context(nc.Block())

        @block.sync
        def _(sp):
            sp.dma_start(raw["wup"][:], wup.rearrange("(k p) f -> p k f", p=P)).then_inc(weights_loaded, 16)
            sp.dma_start(raw["wdn"][:], wdn.rearrange("(k p) d -> p k d", p=P)).then_inc(weights_loaded, 16)
            for name, source in sources.items():
                sp.dma_start(c[name][:], source).then_inc(constants_loaded, 16)
            sp.wait_ge(constants_loaded, 16 * len(sources))

        @block.gpsimd
        def _(pool):
            nc.gpsimd.memset(vx[:], 1.0)
            nc.gpsimd.memset(c["halfs"][:], 0.5)

        @block.tensor
        def _(pe):
            pe.wait_ge(filled, 1)
            pe.wait_ge(summed, 2)
            nc.tensor.matmul(total[:], c["ones"][:], sums[:], start=True, stop=True).then_inc(totalled, 1)

        @block.vector
        def _(dve):
            nc.vector.memset(c["ones"][:], 1.0).then_inc(filled, 1)
            dve.wait_ge(weights_loaded, 32)
            for i, name in enumerate(("wup", "wdn")):
                nc.vector.tensor_reduce(sums[:, i:i + 1], raw[name][:], AX.X, ALU.add,
                                        apply_absolute_value=True).then_inc(summed, 1)
            dve.wait_ge(totalled, 1)
            nc.vector.tensor_scalar(limit[:], total[:], 0.5 / (D * F), None, ALU.mult).then_inc(limits, 1)
            nc.vector.tensor_scalar(minus_limit[:], total[:], -0.5 / (D * F), None, ALU.mult).then_inc(limits, 1)
            dve.wait_ge(limits, 2)
            for i, name in enumerate(("wup", "wdn")):
                if i:
                    dve.wait_ge(ternary, 3)
                nc.vector.tensor_scalar(above[:], raw[name][:], limit[:, i:i + 1], None, ALU.is_gt).then_inc(ternary, 1)
                nc.vector.tensor_scalar(below[:], raw[name][:], minus_limit[:, i:i + 1], None,
                                        ALU.is_lt).then_inc(ternary, 1)
                dve.wait_ge(ternary, 3 * i + 2)
                flat = c[name][:].rearrange("p a b -> p (a b)")
                nc.vector.tensor_tensor(flat, above[:], below[:], ALU.subtract).then_inc(ternary, 1)


def project(nc, sem, sb, ctx, B, c, vx, x, parts_d, v_d, gate_d):
    x_s = sb("x_s", [P, 2, NT, D])
    stats = sb("stats", [P, NT, 6])
    mv = sb("mean_var", [P, NT, 2])
    ln = {k: sb(f"ln_{k}", [P, NT]) for k in ("rstd", "rms", "rmse", "r", "c2")}
    ln |= {k: sb(f"ln_{k}", [P, 2, NT]) for k in ("var", "root")}
    xn = sb("xn", [P, NT, D])
    y = sb("y", [P, NT, D])
    y_parts = sb("y_parts", [P, 2, NT, D], F16)
    xT = sb("xT", [P, KD, BT])
    yT = sb("yT", [P, KD, 2, BT], F16)
    ct = sb("ct", [P, 2, BT])
    rot = {n: sb(f"rot_{n}", [P, 4, BT]) for n in "qk"}
    rope = {n: sb(f"rope_{n}", [P, 2, BT]) for n in "qk"}
    full = {n: sb(f"full_{n}", [P, 2, BT]) for n in "qk"}
    rest = {n: sb(f"rest_{n}", [P, 2, BT]) for n in "qk"}
    part = {n: sb(f"part_{n}", [P, 3, 2, BT], BF16) for n in "qk"}
    unused = sb("unused", [1, 1])
    h = sb("h", [P, KF, BT])
    h_parts = sb("h_parts", [P, 2, KF, BT], F16)
    sq = sb("sq", [P, 2, BT])
    sq_sum = sb("sq_sum", [P, BT])
    ms = {k: sb(f"ms_{k}", [P, NT]) for k in ("mean", "rms", "rmse", "r")}
    gate = sb("gate_s", [P, HB, NT, D])
    bank = [ctx.enter_context(nc.psum_tensor(f"bank{i}", [P, BT], F32)) for i in range(BANKS)]

    mm = {k: sem(f"{k}_in_psum") for k in ("ct", "up", "qk", "v", "xT", "yT", "ss", "down")}
    rd = {k: sem(f"{k}_read") for k in ("ct", "up", "qk", "v", "xT", "yT", "ss", "down")}
    READS = {"ct": 2, "up": KF, "qk": 8, "v": NT, "xT": 2, "yT": 2, "ss": 1, "down": NT}
    x_loaded = [sem(f"x_loaded{i}") for i in range(HB)]
    stats_complete = sem("stats_complete")
    stat_done, mv_done, ln_step = sem("stat_done"), sem("mv_done"), sem("ln_step")
    xn_ready, y_ready, yhi_ready, ylo_ready = sem("xn_ready"), sem("y_ready"), sem("yhi_ready"), sem("ylo_ready")
    hhi_ready, hlo_ready, sq_ready, sum_step = sem("hhi_ready"), sem("hlo_ready"), sem("sq_ready"), sem("sum_step")
    rope_ready, full_ready = sem("rope_ready"), sem("full_ready")
    p1_ready, rest_ready, p2_ready, p3_ready = sem("p1_ready"), sem("rest_ready"), sem("p2_ready"), sem("p3_ready")
    rms_ready, rmse_ready, r_ready = sem("rms_ready"), sem("rmse_ready"), sem("r_ready")
    var_ready, roots_ready = sem("var_ready"), sem("roots_ready")
    parts_stored = {name: sem(f"parts_stored_{name}") for name in "qk"}
    v_stored = [sem(f"v_stored{i}") for i in range(HB)]
    gate_stored = [sem(f"gate_stored{i}") for i in range(HB)]
    LN_STEPS = 5
    XN_AFTER = 1

    def read_value(kind, i, n):
        per = READS[kind]
        last = {"v": 2 * i + 2, "down": 2 * i + 2}.get(kind, i + 1)
        return (n + 1 if kind in ("xT", "yT") else n) * per + last

    def wait_for_bank(pe, u, n, first):
        v = u - BANKS
        while USES[v % len(USES)] is None:
            v -= BANKS
        m = n
        if v < 0:
            v, m = v + len(USES), n - 1
            if first and USES[v] not in ("xT", "yT"):
                return
        kind = USES[v]
        pe.wait_ge(rd[kind], read_value(kind, v - USES.index(kind), m))

    block = ctx.enter_context(nc.Block())

    def each_block(eng, body):
        for hf in range(HB):
            body(0, hf, hf, hf == 0)
        with eng.Fori(1, B) as b:
            for hf in range(HB):
                body(b, b * HB + hf, hf, False)

    @block.sync
    def _(sp):
        def load_x(buf, b, hf):
            sp.dma_start(x_s[:, buf], x[b, hf * BT:(hf + 1) * BT, :].rearrange("(t p) d -> p t d", p=P)
                         ).then_inc(x_loaded[buf], 16)

        def body(b, n, hf, b_next, hf_next):
            sp.wait_ge(y_ready, n + 1)
            load_x(hf, b_next, hf_next)
            tokens = slice(hf * BT, (hf + 1) * BT)
            for name, k in (("q", 0), ("k", 1)):
                for i, ready in enumerate((p1_ready, p2_ready, p3_ready)):
                    sp.wait_ge(ready, 2 * n + k + 1)
                    sp.dma_start(parts_d[name][b, i].rearrange("e p t -> p e t")[:, :, tokens],
                                 part[name][:, i]).then_inc(parts_stored[name], 16)
            sp.wait_ge(rd["v"], NT * (n + 1))
            sp.dma_start(v_d[b, tokens].rearrange("(t p) h c -> p t (h c)", p=P),
                         vx[:, hf].rearrange("p t h c -> p t (h c)")).then_inc(v_stored[hf], 16)
            sp.wait_ge(rd["down"], NT * (n + 1))
            sp.dma_start(gate_d[b, tokens].rearrange("(t p) d -> p t d", p=P), gate[:, hf]).then_inc(gate_stored[hf], 16)

        load_x(0, 0, 0)
        load_x(1, 0, 1)
        with sp.Fori(0, B - 1) as b:
            for hf in range(HB):
                body(b, b * HB + hf, hf, b + 1, hf)
        for hf in range(HB):
            body(B - 1, (B - 1) * HB + hf, hf, B - 1, HB - 1)
        for hf in range(HB):
            sp.wait_ge(x_loaded[hf], 16 * (B + 1))
            sp.wait_ge(v_stored[hf], 16 * B)
            sp.wait_ge(gate_stored[hf], 16 * B)
        for name in "qk":
            sp.wait_ge(parts_stored[name], 16 * 3 * HB * B)

    @block.tensor
    def _(pe):
        def transposes(m, n, first):
            pe.wait_ge(xn_ready, m + 1)
            u = USES.index("xT")
            for k in range(KD):
                if n is not None:
                    wait_for_bank(pe, u + k, n, first)
                for t in range(NT):
                    last = nc.tensor.transpose(bank[(u + k) % BANKS][:, t * P:(t + 1) * P],
                                               xn[:, t, k * P:(k + 1) * P], c["eye32"][:])
                last.then_inc(mm["xT"], 1)
            pe.wait_ge(ylo_ready, m + 1)
            u = USES.index("yT")
            for k in range(KD):
                if n is not None:
                    wait_for_bank(pe, u + k, n, first)
                ps = bank[(u + k) % BANKS][:].bitcast(F16).rearrange("p (a t) -> p a t", a=2)
                for i in range(2):
                    for t in range(NT):
                        last = nc.tensor.transpose(ps[:, i, t * P:(t + 1) * P], y_parts[:, i, t, k * P:(k + 1) * P],
                                                   c["eye16"][:])
                last.then_inc(mm["yT"], 1)

        def body(b, n, hf, first):
            def product(kind, i, pairs, width=BT, at=0, done=True, wait=True):
                u = USES.index(kind) + i
                if wait:
                    wait_for_bank(pe, u, n, first)
                for j, (w, m) in enumerate(pairs):
                    last = nc.tensor.matmul(bank[u % BANKS][:, at:at + width], w, m, start=(j == 0),
                                            stop=(j == len(pairs) - 1))
                if done:
                    last.then_inc(mm[kind], 1)

            pe.wait_ge(rd["xT"], 2 * n + 2)
            for i, w in enumerate(("wdq", "wdkv")):
                product("ct", i, [(c[w][:, k], xT[:, k]) for k in range(KD)])
            pe.wait_ge(rd["yT"], 2 * n + 2)
            for f in range(KF):
                product("up", f, [(c["wup"][:, k, f * P:(f + 1) * P], yT[:, k, i]) for k in range(KD)
                                  for i in range(2)])
            pe.wait_ge(rd["ct"], 2 * n + 2)
            for e in range(2):
                product("qk", e, [(c["wqr"][:, e], ct[:, 0])])
            for e in range(2):
                product("qk", 2 + e, [(c["wkr"][:, k, e], xT[:, k]) for k in range(KD)])
            for e in range(2):
                product("qk", 4 + e, [(c["wuq"][:, e], ct[:, 0])])
            for e in range(2):
                product("qk", 6 + e, [(c["wuk"][:, e], ct[:, 1])])
            pe.wait_ge(sum_step, (KF - 1) * (n + 1))
            u = USES.index("ss")
            wait_for_bank(pe, u, n, first)
            for t in range(NT):
                last = nc.tensor.matmul(bank[u % BANKS][:, t:t + 1], sq_sum[:, t * P:(t + 1) * P],
                                        c["ones"][:, 0:1], start=True, stop=True)
            last.then_inc(mm["ss"], 1)
            pe.wait_ge(hlo_ready, KF * (n + 1))
            for t in range(NT):
                product("down", t // 2, [(h_parts[:, i, f, t * P:(t + 1) * P], c["wdn"][:, f]) for f in range(KF)
                                         for i in range(2)], D, (t % 2) * D, t % 2 == 1, t % 2 == 0)
            transposes(n + 1, n, first)
            for t in range(NT):
                product("v", t // 2, [(ct[:, 1, t * P:(t + 1) * P], c["wuv"][:])], D, (t % 2) * D,
                        t % 2 == 1, t % 2 == 0)

        transposes(0, None, True)
        each_block(pe, body)

    @block.scalar
    def _(act):
        def read_yT(m):
            u = USES.index("yT")
            for k in range(KD):
                act.wait_ge(mm["yT"], 2 * m + k + 1)
                nc.scalar.copy(yT[:, k].rearrange("p a t -> p (a t)"), bank[(u + k) % BANKS][:].bitcast(F16)
                               ).then_inc(rd["yT"], 1)

        def want_table(function):
            nc.scalar.activation(unused[:], c["ones"][0:1, 0:1], function)

        def upper_part(m, first):
            act.wait_ge(y_ready, m + 1)
            if not first:
                act.wait_ge(mm["yT"], 2 * m)
            nc.scalar.copy(y_parts[:, 0], y[:]).then_inc(yhi_ready, 1)

        def body(b, n, hf, first):
            for i, bias in enumerate(("bdq", "bdkv")):
                act.wait_ge(mm["ct"], 2 * n + i + 1)
                nc.scalar.activation(ct[:, i], bank[USES.index("ct") + i][:], ACT.Identity, bias=c[bias][:]
                                     ).then_inc(rd["ct"], 1)
            for f in range(KF):
                act.wait_ge(mm["up"], KF * n + f + 1)
                if not first:
                    act.wait_ge(hlo_ready, KF * n - KF + f + 1)
                nc.scalar.activation(h[:, f], bank[(USES.index("up") + f) % BANKS][:], ACT.Gelu
                                     ).then_inc(rd["up"], 1)
                act.wait_ge(rd["up"], KF * n + f + 1)
                if f == 0:
                    nc.scalar.activation(sq_sum[:], h[:, f], ACT.Square).then_inc(sq_ready, 1)
                else:
                    if f > 2:
                        act.wait_ge(sum_step, (KF - 1) * n + f - 2)
                    nc.scalar.activation(sq[:, f % 2], h[:, f], ACT.Square).then_inc(sq_ready, 1)
            upper_part(n + 1, False)
            want_table(ACT.Silu)
            for j, name in enumerate("qk"):
                act.wait_ge(rd["qk"], 8 * n + 6 + 2 * j)
                if not first:
                    act.wait_ge(parts_stored[name], 48 * n)
                nc.scalar.copy(part[name][:, 0], full[name][:]).then_inc(p1_ready, 1)
            for j, name in enumerate("qk"):
                act.wait_ge(rest_ready, 2 * n + j + 1)
                nc.scalar.copy(part[name][:, 1], rest[name][:]).then_inc(p2_ready, 1)
            act.wait_ge(r_ready, n + 1)
            if not isinstance(b, int):
                act.wait_ge(gate_stored[hf], 16 * b)
            for t in range(NT):
                act.wait_ge(mm["down"], 2 * n + t // 2 + 1)
                u = USES.index("down") + t // 2
                nc.scalar.activation(gate[:, hf, t], bank[u % BANKS][:, (t % 2) * D:(t % 2 + 1) * D], ACT.Silu,
                                     scale=ms["r"][:, t:t + 1]).then_inc(rd["down"], 1)
            want_table(ACT.Gelu)
            read_yT(n + 1)

        upper_part(0, True)
        read_yT(0)
        each_block(act, body)

    @block.vector
    def _(dve):
        def statistics(m, buf, loads):
            dve.wait_ge(x_loaded[buf], 16 * loads)
            for t in range(NT):
                nc.vector.bn_stats(stats[:, t], x_s[:, buf, t]).then_inc(stat_done, 1)
            dve.wait_ge(stat_done, NT * m + NT)
            dve.sem_inc(stats_complete)
            for t in range(NT):
                nc.vector.bn_aggr(mv[:, t], stats[:, t]).then_inc(mv_done, 1)

        def variances(m):
            dve.wait_ge(mv_done, NT * m + NT)
            nc.vector.tensor_copy(ln["var"][:, 0], mv[:, :, 1]).then_inc(var_ready, 1)
            nc.vector.tensor_scalar(ln["var"][:, 1], mv[:, :, 1], LN_EPS, None, ALU.add).then_inc(var_ready, 1)

        def factors(m):
            at = LN_STEPS * m
            dve.wait_ge(roots_ready, m + 1)
            nc.vector.reciprocal(ln["rstd"][:], ln["root"][:, 1]).then_inc(ln_step, 1)
            dve.wait_ge(ln_step, at + 1)
            nc.vector.tensor_tensor(ln["rms"][:], ln["root"][:, 0], ln["rstd"][:], ALU.mult).then_inc(ln_step, 1)
            dve.wait_ge(ln_step, at + 2)
            nc.vector.tensor_scalar(ln["rmse"][:], ln["rms"][:], RMS_EPS, None, ALU.add).then_inc(ln_step, 1)
            dve.wait_ge(ln_step, at + 3)
            nc.vector.reciprocal(ln["r"][:], ln["rmse"][:]).then_inc(ln_step, 1)
            dve.wait_ge(ln_step, at + 4)
            nc.vector.tensor_tensor(ln["c2"][:], ln["rstd"][:], ln["r"][:], ALU.mult).then_inc(ln_step, 1)

        def normalise(m, buf, first):
            dve.wait_ge(ln_step, LN_STEPS * m + LN_STEPS)
            if not first:
                dve.wait_ge(mm["xT"], 2 * m)
            for t in range(NT):
                last = nc.vector.tensor_scalar(xn[:, t], x_s[:, buf, t], mv[:, t, 0:1], ln["rstd"][:, t:t + 1],
                                               ALU.subtract, ALU.mult)
            last.then_inc(xn_ready, 1)
            if not first:
                dve.wait_ge(ylo_ready, m)
            for t in range(NT):
                last = nc.vector.tensor_scalar(y[:, t], x_s[:, buf, t], mv[:, t, 0:1], ln["c2"][:, t:t + 1],
                                               ALU.subtract, ALU.mult)
            last.then_inc(y_ready, 1)

        def lower_part(m):
            dve.wait_ge(yhi_ready, m + 1)
            nc.vector.tensor_tensor(y_parts[:, 1], y[:], y_parts[:, 0], ALU.subtract).then_inc(ylo_ready, 1)

        def read_xT(m):
            u = USES.index("xT")
            for k in range(KD):
                dve.wait_ge(mm["xT"], 2 * m + k + 1)
                nc.vector.tensor_copy(xT[:, k], bank[(u + k) % BANKS][:]).then_inc(rd["xT"], 1)

        def split(n, f):
            dve.wait_ge(rd["up"], KF * n + f + 1)
            nc.vector.tensor_copy(h_parts[:, 0, f], h[:, f]).then_inc(hhi_ready, 1)
            dve.wait_ge(hhi_ready, KF * n + f + 1)
            nc.vector.tensor_tensor(h_parts[:, 1, f], h[:, f], h_parts[:, 0, f], ALU.subtract).then_inc(hlo_ready, 1)

        def body(b, n, hf, first):
            for f in range(KF - 2):
                split(n, f)
                if f == XN_AFTER:
                    normalise(n + 1, (hf + 1) % 2, False)
            tokens = slice(hf * BT, (hf + 1) * BT)
            u = USES.index("qk")
            for j, (name, bias) in enumerate((("q", "bqr"), ("k", "bkr"))):
                if not first:
                    dve.wait_ge(rope_ready, 4 * n - 2 + 2 * j)
                for e in range(2):
                    i = 2 * j + e
                    dve.wait_ge(mm["qk"], 8 * n + i + 1)
                    ps = bank[(u + i) % BANKS][:]
                    b_ = c[bias][:, e:e + 1]
                    nc.vector.scalar_tensor_tensor(rot[name][:, 2 * e], ps, b_, c["cos" if e == 0 else "sin"][:, tokens],
                                                   ALU.add, ALU.mult)
                    nc.vector.scalar_tensor_tensor(rot[name][:, 2 * e + 1], ps, b_,
                                                   c["sin" if e == 0 else "cos"][:, tokens], ALU.add, ALU.mult
                                                   ).then_inc(rd["qk"], 1)
                if j == 0:
                    split(n, KF - 2)
                    split(n, KF - 1)
            for j, (name, bias) in enumerate((("q", "buq"), ("k", "buk"))):
                if not first:
                    dve.wait_ge(rest_ready, 2 * n - 1 + j)
                for e in range(2):
                    i = 4 + 2 * j + e
                    dve.wait_ge(mm["qk"], 8 * n + i + 1)
                    dve.wait_ge(rope_ready, 4 * n + 2 * j + e + 1)
                    nc.vector.scalar_tensor_tensor(full[name][:, e], bank[(u + i) % BANKS][:], c[bias][:, e:e + 1],
                                                   rope[name][:, e], ALU.add, ALU.add).then_inc(rd["qk"], 1)
            lower_part(n + 1)
            dve.wait_ge(mm["ss"], n + 1)
            nc.vector.tensor_scalar(ms["mean"][:], bank[USES.index("ss") % BANKS][:, 0:NT], 1.0 / F, None, ALU.mult
                                    ).then_inc(rd["ss"], 1)
            statistics(n + 2, hf, b + 2)
            variances(n + 2)
            dve.wait_ge(rms_ready, n + 1)
            nc.vector.tensor_scalar(ms["rmse"][:], ms["rms"][:], RMS_EPS, None, ALU.add).then_inc(rmse_ready, 1)
            dve.wait_ge(rmse_ready, n + 1)
            if not first:
                dve.wait_ge(rd["down"], NT * n)
            nc.vector.reciprocal(ms["r"][:], ms["rmse"][:]).then_inc(r_ready, 1)
            read_xT(n + 1)
            for t in range(NT):
                if t == 0 and not isinstance(b, int):
                    dve.wait_ge(v_stored[hf], 16 * b)
                dve.wait_ge(mm["v"], 2 * n + t // 2 + 1)
                ps = bank[(USES.index("v") + t // 2) % BANKS][:, (t % 2) * D:(t % 2 + 1) * D]
                nc.vector.tensor_tensor(vx[:, hf, t, :, 0:HD], ps.rearrange("p (h c) -> p h c", c=HD),
                                        c["buv"][:].rearrange("p (h c) -> p h c", c=HD), ALU.add
                                        ).then_inc(rd["v"], 1)
            factors(n + 2)

        statistics(0, 0, 1)
        variances(0)
        factors(0)
        normalise(0, 0, True)
        lower_part(0)
        statistics(1, 1, 1)
        variances(1)
        factors(1)
        read_xT(0)
        each_block(dve, body)

    @block.gpsimd
    def _(pool):
        def roots(m):
            pool.wait_ge(var_ready, 2 * m + 2)
            nc.gpsimd.tensor_tensor(ln["root"][:], ln["var"][:], c["halfs"][:], ALU.pow).then_inc(roots_ready, 1)

        def body(b, n, hf, first):
            for f in range(1, KF):
                pool.wait_ge(sq_ready, KF * n + f + 1)
                if f > 1:
                    pool.wait_ge(sum_step, (KF - 1) * n + f - 1)
                nc.gpsimd.tensor_tensor(sq_sum[:], sq_sum[:], sq[:, f % 2], ALU.add).then_inc(sum_step, 1)
            for j, name in enumerate("qk"):
                r = rot[name]
                pool.wait_ge(rd["qk"], 8 * n + 2 * j + 2)
                if not first:
                    pool.wait_ge(p1_ready, 2 * n)
                nc.gpsimd.tensor_tensor(rope[name][:, 0], r[:, 0], r[:, 2], ALU.subtract).then_inc(rope_ready, 1)
                nc.gpsimd.tensor_tensor(rope[name][:, 1], r[:, 3], r[:, 1], ALU.add).then_inc(rope_ready, 1)
            for j, name in enumerate("qk"):
                if j:
                    pool.wait_ge(rd["ss"], n + 1)
                    nc.gpsimd.tensor_tensor(ms["rms"][:], ms["mean"][:], c["halfs"][:, 0], ALU.pow
                                            ).then_inc(rms_ready, 1)
                pool.wait_ge(p1_ready, 2 * n + j + 1)
                if not first:
                    pool.wait_ge(p3_ready, 2 * n - 1 + j)
                nc.gpsimd.tensor_tensor(rest[name][:], full[name][:], part[name][:, 0], ALU.subtract
                                        ).then_inc(rest_ready, 1)
            for j, name in enumerate("qk"):
                pool.wait_ge(p2_ready, 2 * n + j + 1)
                nc.gpsimd.tensor_tensor(part[name][:, 2], rest[name][:], part[name][:, 1], ALU.subtract
                                        ).then_inc(p3_ready, 1)
                if j == 0:
                    roots(n + 2)

        roots(0)
        roots(1)
        each_block(pool, body)


def attend(nc, semaphore, ctx, exact, repeat, B, x, wo, bo, parts_d, v_d, gate_d, negmax_d, den_d, rden_d, out):
    suffix = "_exact" if exact else ""

    def sem(name):
        return semaphore(name + suffix)

    def sb(name, shape, dt=F32):
        return ctx.enter_context(nc.sbuf_tensor(name + suffix, shape, dt))

    stack = {n: sb(f"stack_{n}", [ROWS + 1, NG, GH, S], BF16) for n in "qk"}
    v_s = sb("v_s", [P, NG, KT, GH, 2 * HD])
    probs = sb("probs", [P, 2, GH, S])
    maxima = sb("maxima", [P, 2, GH * QT, 2])
    negmax = sb("negmax_s", [P, 2, GH * QT], BF16)
    negmax_t = sb("negmax_t", [P, 2, GH * QT], BF16)
    raw = sb("raw", [P, 2, S])
    o = sb("o", [P, KD, S])
    den = sb("den_s", [P, P])
    rden = sb("rden_s", [P, P])
    rden_b = sb("rden_b", [P, KD, S])
    wo_s = sb("wo_s", [P, KD, D])
    bo_s = sb("bo_s", [P, D])
    res = sb("res", [P, 2, NT, D])
    x_r = sb("x_r", [P, 2, NT, D])
    gate_r = sb("gate_r", [P, 2, NT, D])
    scores = ctx.enter_context(nc.psum_tensor("scores" + suffix, [P, 2, S], F32))
    for_max = ctx.enter_context(nc.psum_tensor("for_max" + suffix, [P, 2, BT], F32))
    sums = ctx.enter_context(nc.psum_tensor("sums" + suffix, [P, S], F32))

    loaded2, ones_set = sem("wo_loaded"), sem("ones_set")
    stack_loaded = [sem(f"stack_loaded{g}") for g in range(NG)]
    st_full, exp_done, pv_done, evacuated = sem("st_full"), sem("exp_done"), sem("pv_done"), sem("evacuated")
    max_full, max_free = sem("max_full"), sem("max_free")
    negmax_ready, negmax_turned = sem("negmax_ready"), sem("negmax_turned")
    negmax_out, shift_loaded = sem("negmax_out"), sem("shift_loaded")
    heads_placed = [sem(f"heads_placed{i}") for i in range(2)]
    den_loaded = sem("den_loaded")
    rden_ready, rden_out, rden_loaded = sem("rden_ready"), sem("rden_out"), sem("rden_loaded")
    o_ready, y_full, y_read, res_step = sem("o_ready"), sem("y_full"), sem("y_read"), sem("res_step")
    sync_passed = sem("sync_passed")
    xg_loaded, out_stored = sem("xg_loaded"), sem("out_stored")
    STACK_DMAS = 2 * 2 * len(TERMS) + 1
    INVERT_AT = 3
    HEAD_TILES = 4
    UNIT = HEAD_TILES * 2 if exact else 1
    worst = sb("worst", [P, 2])
    over = sb("over", [P, 1])
    ones = sb("ones_2", [P, P])
    worst_step, over_ready, over_total = sem("worst_step"), sem("over_ready"), sem("over_total")
    repeat_ready = sem("repeat_ready")

    def when_wanted(eng, program):
        if exact:
            with eng.If(eng.value_load(repeat[0:1, 0:1], min_val=0, max_val=P) > 0):
                program()
        else:
            program()

    block = ctx.enter_context(nc.Block())

    def ahead(g, s):
        u = g * KT + s + LEAD
        return u // (NG * KT), (u // KT) % NG, u % KT

    @block.sync
    def _(sp):
        def wait(what, value):
            sp.wait_ge(what, value)
            sp.sem_inc(sync_passed)

        def load_group(b, g):
            for k, name in enumerate("qk"):
                for t, pair in enumerate(TERMS):
                    for e in range(2):
                        r = t * HD + e * HD // 2
                        rows = parts_d[name][b, pair[k], e, g * GH * HD // 2:(g + 1) * GH * HD // 2, :]
                        sp.dma_start(stack[name][r:r + HD // 2, g], rows.rearrange("(j i) t -> i j t", i=HD // 2)
                                     ).then_inc(stack_loaded[g], 16)
            sp.dma_start(v_s[:, g], v_d[b, :, g * GH:(g + 1) * GH, :].rearrange("(k p) j c -> p k j c", p=P)
                         ).then_inc(stack_loaded[g], 16)

        def shift_rows(b, g):
            G, par = b * NG + g, g % 2
            wait(negmax_turned, G + 1)
            for q in range(4):
                sp.dma_start(negmax_d[par].rearrange("(c q r) -> q c r", q=4, r=32)[q],
                             negmax_t[32 * q:32 * q + 32, par, :]).then_inc(negmax_out, 16)
            wait(negmax_out, G * 64 + 64)
            sp.dma_start(stack["q"][ROWS:ROWS + 1, g].rearrange("p j t -> p (j t)"), negmax_d[par:par + 1, :]
                         ).then_inc(shift_loaded, 16)

        def place_heads(b, g):
            wait(evacuated, b * NG + g + 1)
            for j in range(GH):
                head = g * GH + j
                at = (head * HD) % P
                sp.dma_start(o[at:at + HD, head * HD // P], raw[32 * j:32 * j + HD, g % 2]
                             ).then_inc(heads_placed[g % 2], 16)
            sp.dma_start(den_d[g * GH:(g + 1) * GH, :], raw[HD:P:32, g % 2]).then_inc(heads_placed[g % 2], 16)

        def load_denominators(b):
            for placed in heads_placed:
                wait(placed, 40 * NG * b + 40 * NG)
            sp.dma_start(den[:], den_d.rearrange("h (a c) -> (h a) c", c=P)).then_inc(den_loaded, 16)

        def spread_denominators(b):
            wait(rden_ready, b + 1)
            sp.dma_start(rden_d.rearrange("h (a c) -> (h a) c", c=P), rden[:]).then_inc(rden_out, 16)
            wait(rden_out, 16 * b + 16)
            for i in range(P // HD):
                sp.dma_start(rden_b[i * HD:(i + 1) * HD], rden_d.rearrange("(k h) t -> h k t", k=KD)[i]
                             .partition_broadcast(HD)).then_inc(rden_loaded, 16)

        def load_residual(b):
            for k in range(2):
                tokens = slice(k * BT, (k + 1) * BT)
                sp.dma_start(x_r[:, k], x[b, tokens].rearrange("(t p) d -> p t d", p=P)).then_inc(xg_loaded, 16)
                sp.dma_start(gate_r[:, k], gate_d[b, tokens].rearrange("(t p) d -> p t d", p=P)
                             ).then_inc(xg_loaded, 16)

        def T(b, g, last):
            first = isinstance(b, int) and b == 0 and g == 0
            G = b * NG + g
            if g == 0 and not first:
                place_heads(b - 1, NG - 1)
                load_denominators(b - 1)
                spread_denominators(b - 1)
            if not last:
                if not first:
                    wait(st_full, GH * KT * G)
                    wait(pv_done, KT * G)
                load_group(*((b, 3) if g == 0 else (b + 1, g - 1)))
            elif first:
                load_group(b, 3)
            if g:
                place_heads(b, g - 1)
            if g == NG - 1:
                load_residual(b)
            if g < NG - 1:
                shift_rows(b, g + 1)
            elif not last:
                shift_rows(b + 1, 0)

        def O(b):
            for k in range(2):
                wait(res_step, 6 * b + 3 * k + 3)
                sp.dma_start(out[b, k * BT:(k + 1) * BT].rearrange("(t p) d -> p t d", p=P), res[:, k]
                             ).then_inc(out_stored, 16)

        def last_O(b):
            place_heads(b, NG - 1)
            load_denominators(b)
            spread_denominators(b)
            O(b)

        def program():
            sp.dma_start(wo_s[:], wo.rearrange("(k p) n -> p k n", p=P)).then_inc(loaded2, 16)
            sp.dma_start(bo_s[:], bo.partition_broadcast(P)).then_inc(loaded2, 16)
            for g in range(3):
                load_group(0, g)
            shift_rows(0, 0)
            T(0, 0, B == 1)
            if B > 1:
                with sp.Fori(0, B - 1) as b:
                    for g in range(1, NG):
                        T(b, g, False)
                    T(b + 1, 0, False)
                    O(b)
            for g in range(1, NG):
                T(B - 1, g, True)
            last_O(B - 1)
            wait(out_stored, 32 * B)
            for g in range(NG):
                wait(stack_loaded[g], 16 * STACK_DMAS * B)

        when_wanted(sp, program)

    @block.tensor
    def _(pe):
        def wait_for_stack(b, g, u):
            if u == 0:
                pe.wait_ge(stack_loaded[g], b * 16 * STACK_DMAS + 16 * STACK_DMAS)

        def maxima_products(b, g, u, t):
            j, qt = u // 2, HEAD_TILES * (u % 2) + t
            base = (b * NG + g) * KT * UNIT + u * UNIT
            queries = stack["q"][0:ROWS, g, j, qt * P:(qt + 1) * P]
            if exact:
                for half in range(2):
                    index = base + 2 * t + half
                    if not (isinstance(index, int) and index < 2):
                        pe.wait_ge(max_free, index - 1)
                    nc.tensor.matmul(for_max[:, half], queries, stack["k"][0:ROWS, g, j, half * BT:(half + 1) * BT],
                                     start=True, stop=True).then_inc(max_full, 1)
            else:
                if t == 0 and not (isinstance(base, int) and base < 2):
                    pe.wait_ge(max_free, base - 1)
                mm = nc.tensor.matmul(for_max[:, u % 2, t * S // SAMPLE:(t + 1) * S // SAMPLE], queries,
                                      stack["k"][0:ROWS, g, j, 0:S:SAMPLE], start=True, stop=True)
                if t == HEAD_TILES - 1:
                    mm.then_inc(max_full, 1)

        def pv(b, g, s, half):
            n = (b * NG + g) * KT + s
            if half == 0:
                pe.wait_ge(exp_done, n * GH + GH)
                if s == 0 and not (isinstance(n, int) and n == 0):
                    pe.wait_ge(evacuated, b * NG + g)
            queries = slice(half * BT, (half + 1) * BT)
            for j in range(GH):
                last = nc.tensor.matmul(sums[32 * j:32 * j + 32, queries], v_s[:, g, s, j], probs[:, s % 2, j, queries],
                                        start=(s == 0), stop=(s == KT - 1))
            if half == 1:
                last.then_inc(pv_done, 1)

        def T(b, g, last):
            G = b * NG + g
            first = isinstance(b, int) and b == 0 and g == 0
            pe.wait_ge(shift_loaded, 16 * G + 16)
            for s in range(KT):
                db, mg, u = ahead(g, s)
                more = not (last and db)
                if more:
                    wait_for_stack(b + db, mg, u)
                for j in range(GH):
                    e = G * KT * GH + s * GH + j
                    if not (first and s == 0 and j < 2):
                        pe.wait_ge(exp_done, e - 1)
                    for half in range(2):
                        mm = nc.tensor.matmul(scores[:, j % 2, half * BT:(half + 1) * BT],
                                              stack["k"][:, g, j, s * P:(s + 1) * P],
                                              stack["q"][:, g, j, half * BT:(half + 1) * BT], start=True, stop=True)
                    mm.then_inc(st_full, 1)
                    if more:
                        maxima_products(b + db, mg, u, j)
                    if not (first and s == 0):
                        before = (b, g, s - 1) if s else ((b, g - 1, KT - 1) if g else (b - 1, NG - 1, KT - 1))
                        if j % 2:
                            pv(*before, j // 2)

        def O(b, tail=False):
            if tail:
                for half in range(2):
                    pv(b, NG - 1, KT - 1, half)
                pe.wait_ge(exp_done, GH * KT * NG * (b + 1))
            else:
                pe.wait_ge(exp_done, (b * NG + NG + 1) * KT * GH)
            pe.wait_ge(o_ready, 2 * b + 2)
            for k in range(2):
                for t in range(NT):
                    for i in range(KD):
                        mm = nc.tensor.matmul(scores[:, k, t * D:(t + 1) * D],
                                              o[:, i, (k * NT + t) * P:(k * NT + t + 1) * P], wo_s[:, i],
                                              start=(i == 0), stop=(i == KD - 1))
                mm.then_inc(y_full, 1)
            pe.wait_ge(y_read, 2 * b + 2)

        def program():
            pe.wait_ge(loaded2, 32)
            pe.wait_ge(ones_set, 2)
            for n in range(LEAD):
                wait_for_stack(0, n // KT, n % KT)
                for t in range(HEAD_TILES):
                    maxima_products(0, n // KT, n % KT, t)
            T(0, 0, B == 1)
            if B > 1:
                with pe.Fori(0, B - 1) as b:
                    for g in range(1, NG):
                        T(b, g, False)
                    T(b + 1, 0, False)
                    O(b)
            for g in range(1, NG):
                T(B - 1, g, True)
            O(B - 1, True)
            if not exact:
                pe.wait_ge(over_ready, 1)
                nc.tensor.matmul(for_max[:, 0, 0:1], ones[:], over[:], start=True, stop=True).then_inc(over_total, 1)

        when_wanted(pe, program)

    @block.scalar
    def _(act):
        def T(b, g, last):
            G = b * NG + g
            first = isinstance(b, int) and b == 0 and g == 0
            for s in range(KT):
                n = G * KT + s
                for j in range(GH):
                    e = n * GH + j
                    act.wait_ge(st_full, e + 1)
                    if j == 0 and not (first and s < 2):
                        act.wait_ge(pv_done, n - 1)
                    nc.scalar.activation(probs[:, s % 2, j], scores[:, j % 2], ACT.Exp, scale=SCORE_SCALE
                                         ).then_inc(exp_done, 1)

        def program():
            T(0, 0, B == 1)
            if B > 1:
                with act.Fori(0, B - 1) as b:
                    for g in range(1, NG):
                        T(b, g, False)
                    T(b + 1, 0, False)
            for g in range(1, NG):
                T(B - 1, g, True)

        when_wanted(act, program)

    @block.vector
    def _(dve):
        def reduce_unit(b, g, u):
            G, par = b * NG + g, g % 2
            for i in range(UNIT):
                dve.wait_ge(max_full, G * KT * UNIT + u * UNIT + i + 1)
                if exact:
                    nc.vector.tensor_reduce(maxima[:, par, u * HEAD_TILES + i // 2, i % 2:i % 2 + 1],
                                            for_max[:, i % 2], AX.X, ALU.max).then_inc(max_free, 1)
                else:
                    nc.vector.tensor_reduce(maxima[:, par, u * HEAD_TILES:(u + 1) * HEAD_TILES, 0],
                                            for_max[:, u % 2, 0:HEAD_TILES * S // SAMPLE].rearrange("p (t k) -> p t k", t=HEAD_TILES), AX.X,
                                            ALU.max).then_inc(max_free, 1)
            if u == KT - 1:
                dve.wait_ge(max_free, G * KT * UNIT + KT * UNIT)
                if exact:
                    nc.vector.tensor_reduce(negmax[:, par], maxima[:, par], AX.X, ALU.max, negate=True
                                            ).then_inc(negmax_ready, 1)
                else:
                    nc.vector.tensor_scalar(negmax[:, par], maxima[:, par, :, 0], -1.0, -HEADROOM / SCORE_SCALE,
                                            ALU.mult, ALU.add).then_inc(negmax_ready, 1)
                dve.wait_ge(negmax_ready, G + 1)
                if not (isinstance(b, int) and b == 0 and g < 2):
                    dve.wait_ge(negmax_out, 64 * G - 64)
                nc.vector.transpose(negmax_t[:, par], negmax[:, par]).then_inc(negmax_turned, 1)

        def evacuate(b, g):
            dve.wait_ge(pv_done, (b * NG + g) * KT + KT)
            if g >= 2:
                dve.wait_ge(heads_placed[g % 2], 40 * NG * b + 80)
            nc.vector.tensor_copy(raw[:, g % 2], sums[:]).then_inc(evacuated, 1)

        def invert(b):
            dve.wait_ge(den_loaded, 16 * b + 16)
            nc.vector.reciprocal(rden[:], den[:]).then_inc(rden_ready, 1)
            if not exact:
                nc.vector.tensor_reduce(worst[:, 1:2], den[:], AX.X, ALU.max).then_inc(worst_step, 1)
                dve.wait_ge(worst_step, 2 * b + 2)
                nc.vector.tensor_tensor(worst[:, 0:1], worst[:, 0:1], worst[:, 1:2], ALU.max).then_inc(worst_step, 1)

        def normalise(b, i):
            dve.wait_ge(rden_loaded, 16 * (P // HD) * b + 16 * (P // HD))
            nc.vector.tensor_tensor(o[:, i], o[:, i], rden_b[:, i], ALU.mult).then_inc(o_ready, 1)

        def T(b, g, last):
            first = isinstance(b, int) and b == 0 and g == 0
            for s in range(KT):
                db, mg, u = ahead(g, s)
                if not (last and db):
                    reduce_unit(b + db, mg, u)
                if s == 0 and not first:
                    evacuate(*((b, g - 1) if g else (b - 1, NG - 1)))
                if g == 0 and s == INVERT_AT and not first:
                    invert(b - 1)
                if g == 0 and s >= KT - 2 and not first:
                    normalise(b - 1, s - KT + 2)

        def O(b):
            for k in range(2):
                dve.wait_ge(y_full, 2 * b + k + 1)
                nc.vector.tensor_copy(res[:, k].rearrange("p t d -> p (t d)"), scores[:, k]).then_inc(y_read, 1)

        def program():
            nc.vector.memset(stack["k"][ROWS:ROWS + 1], 1.0).then_inc(ones_set, 1)
            nc.vector.memset(ones[:], 1.0).then_inc(ones_set, 1)
            nc.vector.memset(worst[:], 0.0).then_inc(worst_step, 1)
            for n in range(LEAD):
                reduce_unit(0, n // KT, n % KT)
            T(0, 0, B == 1)
            if B > 1:
                with dve.Fori(0, B - 1) as b:
                    for g in range(1, NG):
                        T(b, g, False)
                    T(b + 1, 0, False)
                    O(b)
            for g in range(1, NG):
                T(B - 1, g, True)
            evacuate(B - 1, NG - 1)
            invert(B - 1)
            for i in range(KD):
                normalise(B - 1, i)
            O(B - 1)
            if not exact:
                dve.wait_ge(worst_step, 2 * B + 1)
                nc.vector.tensor_scalar(over[:], worst[:, 0:1], DEN_LIMIT, None, ALU.is_gt).then_inc(over_ready, 1)
                dve.wait_ge(over_total, 1)
                nc.vector.tensor_copy(repeat[:], for_max[:, 0, 0:1]).then_inc(repeat_ready, 1)

        when_wanted(dve, program)

    @block.gpsimd
    def _(pool):
        def O(b):
            pool.wait_ge(xg_loaded, 64 * b + 64)
            for k in range(2):
                r = res[:, k]
                pool.wait_ge(y_read, 2 * b + k + 1)
                nc.gpsimd.tensor_tensor(r, r, bo_s[:].unsqueeze(1).to_broadcast([P, NT, D]), ALU.add
                                        ).then_inc(res_step, 1)
                pool.wait_ge(res_step, 6 * b + 3 * k + 1)
                nc.gpsimd.tensor_tensor(r, r, gate_r[:, k], ALU.mult).then_inc(res_step, 1)
                pool.wait_ge(res_step, 6 * b + 3 * k + 2)
                nc.gpsimd.tensor_tensor(r, r, x_r[:, k], ALU.add).then_inc(res_step, 1)
            pool.wait_ge(out_stored, 32 * b + 32)

        def program():
            pool.wait_ge(loaded2, 32)
            if B > 1:
                with pool.Fori(0, B - 1) as b:
                    O(b)
            O(B - 1)

        when_wanted(pool, program)


_NAMES = ["x", "wdq", "bdq", "wdkv", "bdkv", "wuq", "buq", "wqr", "bqr", "wkr", "bkr", "wuk", "buk", "wuv", "buv",
          "wo", "bo", "wup", "wdn", "cos", "sin", "eye32", "eye16"]


def lay_out(i):
    def eo(w):
        return np.ascontiguousarray(w.reshape(w.shape[0], D // 2, 2).transpose(0, 2, 1))

    def col(v):
        return np.ascontiguousarray(v.reshape(-1, 1))

    def pair(v):
        return np.ascontiguousarray(v.reshape(D // 2, 2))

    a = {k: np.asarray(v) for k, v in i.items()}
    f = lambda name: a["L0_attn_" + name]
    position = np.arange(S, dtype=np.float32)[:, None]
    ids = np.arange(D // 2, dtype=np.float32)
    theta = (np.float32(10000.0) ** (np.float32(-2.0) * ids)) / np.float32(D // 2)
    angle = (position * theta[None, :]).astype(np.float32)
    return {
        "x": f("x"), "wdq": f("Wd_q_w"), "bdq": col(f("Wd_q_b")), "wdkv": f("Wd_kv_w"), "bdkv": col(f("Wd_kv_b")),
        "wuq": eo(f("Wu_q_w")), "buq": pair(f("Wu_q_b")), "wqr": eo(f("Wq_r_w")), "bqr": pair(f("Wq_r_b")),
        "wkr": eo(f("Wk_r_w")), "bkr": pair(f("Wk_r_b")), "wuk": eo(f("Wu_k_w")), "buk": pair(f("Wu_k_b")),
        "wuv": f("Wu_v_w"), "buv": f("Wu_v_b"), "wo": f("Wo_w"), "bo": f("Wo_b"),
        "wup": np.ascontiguousarray(a["L0_ffn_w_up"].T), "wdn": np.ascontiguousarray(a["L0_ffn_w_down"].T),
        "cos": np.ascontiguousarray(np.cos(angle).T), "sin": np.ascontiguousarray(np.sin(angle).T),
        "eye32": np.eye(P, dtype=np.float32), "eye16": np.eye(P, dtype=np.float16),
    }


def kernel(**inputs):
    import concourse.bacc as bacc
    from concourse.bass_utils import run_bass_kernel_spmd as run

    nc = bacc.Bacc("TRN2", target_bir_lowering=False, num_devices=1)
    laid = lay_out(inputs)
    arrays = {f"in_{n}": np.ascontiguousarray(laid[n]) for n in _NAMES}
    args = [nc.dram_tensor(f"in_{n}", arrays[f"in_{n}"].shape, mybir.dt.from_np(arrays[f"in_{n}"].dtype),
                           kind="ExternalInput").ap() for n in _NAMES]
    out = nc.dram_tensor("out_0", laid["x"].shape, F32, kind="ExternalOutput").ap()
    build_program(nc, *args, out)
    r = run(nc, [arrays], core_ids=[0])
    return r.results[0]["out_0"]
```

```python
from contextlib import ExitStack

import numpy as np

import concourse.bass as bass
from concourse import mybir

F32 = mybir.dt.float32
F16 = mybir.dt.float16
BF16 = mybir.dt.bfloat16
ALU = mybir.AluOpType
ACT = mybir.ActivationFunctionType
AX = mybir.AxisListType

P = 128
S = 1024
D = 256
H = 16
HD = D // H
F = 1024
BT = 512
NT = BT // P
KD = D // P
KF = F // P
HB = S // BT
SCORE_SCALE = float(1.0 / np.sqrt(np.float32(H + 128 + 128)))
LN_EPS = 1e-5
RMS_EPS = 1e-8

TERMS = [(0, 0), (0, 1), (0, 2), (1, 0), (1, 1), (2, 0)]
ROWS = len(TERMS) * HD
GH = 4
NG = H // GH
SAMPLE = 16
HEADROOM = 40.0
DEN_LIMIT = 1e25
KT = S // P
QT = S // P
HEAD_TILES = 2
STEPS = GH * QT // HEAD_TILES
assert STEPS == HB * KT
LEAD = STEPS + 6
RING = 3

BANKS = 7
USES = (["ct"] * 2 + ["up"] * KF + ["qk"] * 8 + ["ss"] + ["down"] * 2 + ["xT"] * 2 + ["yT"] * 2 + ["v"] * 2 + [None])
assert len(USES) % BANKS == 0


def build_program(nc, x, wdq, bdq, wdkv, bdkv, wuq, buq, wqr, bqr, wkr, bkr, wuk, buk, wuv, buv, wo, bo,
                  wup, wdn, cos, sin, eye32, eye16, out):
    B = x.shape[0]
    parts_d = {n: nc.dram_tensor(f"{n}_parts", [B, 3, D, S], BF16).ap() for n in "qk"}
    v_d = nc.dram_tensor("v_ones", [B, S, H, 2 * HD], F32).ap()
    gate_d = nc.dram_tensor("gate", [B, S, D], F32).ap()
    negmax_d = nc.dram_tensor("negmax", [2, GH * S], BF16).ap()
    den_d = nc.dram_tensor("den", [H, S], F32).ap()
    rden_d = nc.dram_tensor("rden", [H, S], F32).ap()

    with ExitStack() as ctx:
        def sem(name):
            return ctx.enter_context(nc.semaphore(name))

        with ExitStack() as part1:
            def sb(name, shape, dt=F32):
                return part1.enter_context(nc.sbuf_tensor(name, shape, dt))

            c = {
                "wdq": sb("wdq_s", [P, KD, P]), "wdkv": sb("wdkv_s", [P, KD, P]),
                "wuq": sb("wuq_s", [P, 2, P]), "wqr": sb("wqr_s", [P, 2, P]),
                "wkr": sb("wkr_s", [P, KD, 2, P]), "wuk": sb("wuk_s", [P, 2, P]),
                "wuv": sb("wuv_s", [P, D]), "buv": sb("buv_s", [P, D]),
                "bdq": sb("bdq_s", [P, 1]), "bdkv": sb("bdkv_s", [P, 1]),
                "buq": sb("buq_s", [P, 2]), "bqr": sb("bqr_s", [P, 2]),
                "bkr": sb("bkr_s", [P, 2]), "buk": sb("buk_s", [P, 2]),
                "cos": sb("cos_s", [P, S]), "sin": sb("sin_s", [P, S]),
                "eye32": sb("eye32_s", [P, P]), "eye16": sb("eye16_s", [P, P], F16),
                "wup": sb("wup_t", [P, KD, F], F16), "wdn": sb("wdn_t", [P, KF, D], F16),
                "ones": sb("ones_s", [P, P]), "halfs": sb("halfs", [P, 2, NT]),
            }
            vx = sb("vx", [P, HB, NT, H, 2 * HD])
            sources = {
                "wdq": wdq.rearrange("(k p) m -> p k m", p=P), "wdkv": wdkv.rearrange("(k p) m -> p k m", p=P),
                "wuq": wuq, "wqr": wqr, "wkr": wkr.rearrange("(k p) e m -> p k e m", p=P), "wuk": wuk,
                "wuv": wuv, "buv": buv.partition_broadcast(P), "bdq": bdq, "bdkv": bdkv, "buq": buq,
                "bqr": bqr, "bkr": bkr, "buk": buk, "cos": cos, "sin": sin, "eye32": eye32, "eye16": eye16,
            }
            project(nc, sem, sb, part1, B, c, vx, sources, wup, wdn, x, parts_d, v_d, gate_d)
        repeat = ctx.enter_context(nc.sbuf_tensor("repeat", [P, 1], mybir.dt.int32))
        for exact in (False, True):
            with ExitStack() as part2:
                attend(nc, sem, part2, exact, repeat, B, x, wo, bo, parts_d, v_d, gate_d, negmax_d, den_d, rden_d,
                       out)


def project(nc, sem, sb, ctx, B, c, vx, sources, wup, wdn, x, parts_d, v_d, gate_d):
    raw = {"wup": sb("wup_raw", [P, KD * F]), "wdn": sb("wdn_raw", [P, KF * D])}
    below = sb("below", [P, KD * F])
    sums = sb("abs_sums", [P, 2])
    limit = sb("limit", [P, 2])
    minus_limit = sb("minus_limit", [P, 2])
    weights_loaded, constants_loaded = {n: sem(f"{n}_loaded") for n in raw}, sem("constants_loaded")
    eyes_loaded, filled = sem("eyes_loaded"), sem("filled")
    halfs_filled, vx_filled = sem("halfs_filled"), sem("vx_filled")
    summed, totalled, limits, ternary = sem("abs_summed"), sem("abs_totalled"), sem("limits"), sem("ternary")
    CONSTANTS_DONE = 16 * (len(sources) - 2)
    x_s = sb("x_s", [P, 2, NT, D])
    stats = sb("stats", [P, NT, 6])
    mv = sb("mean_var", [P, NT, 2])
    ln = {k: sb(f"ln_{k}", [P, NT]) for k in ("rstd", "rms", "rmse", "r", "c2")}
    ln |= {k: sb(f"ln_{k}", [P, 2, NT]) for k in ("var", "root")}
    xn = sb("xn", [P, NT, D])
    y = sb("y", [P, NT, D])
    y_parts = sb("y_parts", [P, 2, NT, D], F16)
    xT = sb("xT", [P, KD, BT])
    yT = sb("yT", [P, KD, 2, BT], F16)
    ct = sb("ct", [P, 2, BT])
    rot = {n: sb(f"rot_{n}", [P, 4, BT]) for n in "qk"}
    rope = {n: sb(f"rope_{n}", [P, 2, BT]) for n in "qk"}
    full = {n: sb(f"full_{n}", [P, 2, BT]) for n in "qk"}
    rest = {n: sb(f"rest_{n}", [P, 2, BT]) for n in "qk"}
    part = {n: sb(f"part_{n}", [P, 3, 2, BT], BF16) for n in "qk"}
    unused = sb("unused", [1, 1])
    h = sb("h", [P, KF, BT])
    h_parts = sb("h_parts", [P, 2, KF, BT], F16)
    sq = sb("sq", [P, 2, BT])
    sq_sum = sb("sq_sum", [P, BT])
    ms = {k: sb(f"ms_{k}", [P, NT]) for k in ("mean", "rms", "rmse", "r")}
    gate = sb("gate_s", [P, HB, NT, D])
    total = ctx.enter_context(nc.psum_tensor("abs_total", [P, BT], F32))
    bank = [ctx.enter_context(nc.psum_tensor(f"bank{i}", [P, BT], F32)) for i in range(BANKS)]

    mm = {k: sem(f"{k}_in_psum") for k in ("ct", "up", "qk", "v", "xT", "yT", "ss", "down")}
    rd = {k: sem(f"{k}_read") for k in ("ct", "up", "qk", "v", "xT", "yT", "ss", "down")}
    READS = {"ct": 2, "up": KF, "qk": 8, "v": NT, "xT": 2, "yT": 2, "ss": 1, "down": NT}
    x_loaded = [sem(f"x_loaded{i}") for i in range(HB)]
    stats_complete = sem("stats_complete")
    stat_done, mv_done, ln_step = sem("stat_done"), sem("mv_done"), sem("ln_step")
    xn_ready, y_ready, yhi_ready, ylo_ready = sem("xn_ready"), sem("y_ready"), sem("yhi_ready"), sem("ylo_ready")
    last_hhi_ready = sem("last_hhi_ready")
    hhi_ready, hlo_ready, sq_ready, sum_step = sem("hhi_ready"), sem("hlo_ready"), sem("sq_ready"), sem("sum_step")
    rope_ready, full_ready = sem("rope_ready"), sem("full_ready")
    p1_ready, rest_ready, p2_ready, p3_ready = sem("p1_ready"), sem("rest_ready"), sem("p2_ready"), sem("p3_ready")
    rms_ready, rmse_ready, r_ready = sem("rms_ready"), sem("rmse_ready"), sem("r_ready")
    var_ready, roots_ready = sem("var_ready"), sem("roots_ready")
    parts_stored = {name: sem(f"parts_stored_{name}") for name in "qk"}
    v_stored = [sem(f"v_stored{i}") for i in range(HB)]
    gate_stored = [sem(f"gate_stored{i}") for i in range(HB)]
    LN_STEPS = 5
    XN_AFTER = 1

    def read_value(kind, i, n):
        per = READS[kind]
        last = {"v": 2 * i + 2, "down": 2 * i + 2}.get(kind, i + 1)
        return (n + 1 if kind in ("xT", "yT") else n) * per + last

    def wait_for_bank(pe, u, n, first):
        v = u - BANKS
        while USES[v % len(USES)] is None:
            v -= BANKS
        m = n
        if v < 0:
            v, m = v + len(USES), n - 1
            if first and USES[v] not in ("xT", "yT"):
                return
        kind = USES[v]
        pe.wait_ge(rd[kind], read_value(kind, v - USES.index(kind), m))

    block = ctx.enter_context(nc.Block())

    def each_block(eng, body):
        for hf in range(HB):
            body(0, hf, hf, hf == 0)
        with eng.Fori(1, B) as b:
            for hf in range(HB):
                body(b, b * HB + hf, hf, False)

    @block.sync
    def _(sp):
        def load_x(buf, b, hf):
            sp.dma_start(x_s[:, buf], x[b, hf * BT:(hf + 1) * BT, :].rearrange("(t p) d -> p t d", p=P)
                         ).then_inc(x_loaded[buf], 16)

        def body(b, n, hf, b_next, hf_next):
            sp.wait_ge(y_ready, n + 1)
            load_x(hf, b_next, hf_next)
            tokens = slice(hf * BT, (hf + 1) * BT)

            def store_part(name, i, ready):
                sp.wait_ge(ready, 2 * n + "qk".index(name) + 1)
                rows = parts_d[name][b, i].rearrange("(h e j) t -> h e j t", h=H, e=2)
                for e in range(2):
                    sp.dma_start(rows[:, e, :, tokens], part[name][:, i, e]).then_inc(parts_stored[name], 16)

            for i, ready in enumerate((p1_ready, p2_ready)):
                for name in "qk":
                    store_part(name, i, ready)
            sp.wait_ge(rd["down"], NT * (n + 1))
            sp.dma_start(gate_d[b, tokens].rearrange("(t p) d -> p t d", p=P), gate[:, hf]
                         ).then_inc(gate_stored[hf], 16)
            sp.wait_ge(rd["v"], NT * (n + 1))
            sp.dma_start(v_d[b, tokens].rearrange("(t p) h c -> p t (h c)", p=P),
                         vx[:, hf].rearrange("p t h c -> p t (h c)")).then_inc(v_stored[hf], 16)
            for name in "qk":
                store_part(name, 2, p3_ready)

        load_x(0, 0, 0)
        for name in ("eye32", "eye16"):
            sp.dma_start(c[name][:], sources[name]).then_inc(eyes_loaded, 16)
        sp.dma_start(raw["wup"][:], wup.rearrange("(k p) f -> p k f", p=P)).then_inc(weights_loaded["wup"], 16)
        sp.dma_start(raw["wdn"][:], wdn.rearrange("(k p) d -> p k d", p=P)).then_inc(weights_loaded["wdn"], 16)
        for name, source in sources.items():
            if name not in ("eye32", "eye16"):
                sp.dma_start(c[name][:], source).then_inc(constants_loaded, 16)
        load_x(1, 0, 1)
        with sp.Fori(0, B - 1) as b:
            for hf in range(HB):
                body(b, b * HB + hf, hf, b + 1, hf)
        for hf in range(HB):
            body(B - 1, (B - 1) * HB + hf, hf, B - 1, HB - 1)
        for hf in range(HB):
            sp.wait_ge(x_loaded[hf], 16 * (B + 1))
            sp.wait_ge(v_stored[hf], 16 * B)
            sp.wait_ge(gate_stored[hf], 16 * B)
        for name in "qk":
            sp.wait_ge(parts_stored[name], 96 * HB * B)

    @block.tensor
    def _(pe):
        def transposes(m, n, first):
            pe.wait_ge(xn_ready, m + 1)
            u = USES.index("xT")
            for k in range(KD):
                if n is not None:
                    wait_for_bank(pe, u + k, n, first)
                for t in range(NT):
                    last = nc.tensor.transpose(bank[(u + k) % BANKS][:, t * P:(t + 1) * P],
                                               xn[:, t, k * P:(k + 1) * P], c["eye32"][:])
                last.then_inc(mm["xT"], 1)
            pe.wait_ge(ylo_ready, m + 1)
            u = USES.index("yT")
            for k in range(KD):
                if n is not None:
                    wait_for_bank(pe, u + k, n, first)
                ps = bank[(u + k) % BANKS][:].bitcast(F16).rearrange("p (a t) -> p a t", a=2)
                for i in range(2):
                    for t in range(NT):
                        last = nc.tensor.transpose(ps[:, i, t * P:(t + 1) * P], y_parts[:, i, t, k * P:(k + 1) * P],
                                                   c["eye16"][:])
                last.then_inc(mm["yT"], 1)

        def body(b, n, hf, first):
            def product(kind, i, pairs, width=BT, at=0, done=True, wait=True):
                u = USES.index(kind) + i
                if wait:
                    wait_for_bank(pe, u, n, first)
                for j, (w, m) in enumerate(pairs):
                    last = nc.tensor.matmul(bank[u % BANKS][:, at:at + width], w, m, start=(j == 0),
                                            stop=(j == len(pairs) - 1))
                if done:
                    last.then_inc(mm[kind], 1)

            if first:
                pe.wait_ge(constants_loaded, CONSTANTS_DONE)
            pe.wait_ge(rd["xT"], 2 * n + 2)
            for i, w in enumerate(("wdq", "wdkv")):
                product("ct", i, [(c[w][:, k], xT[:, k]) for k in range(KD)])
            pe.wait_ge(rd["yT"], 2 * n + 2)
            if first:
                pe.wait_ge(ternary, 2)
            for f in range(KF):
                product("up", f, [(c["wup"][:, k, f * P:(f + 1) * P], yT[:, k, i]) for k in range(KD)
                                  for i in range(2)])
            pe.wait_ge(rd["ct"], 2 * n + 2)
            for e in range(2):
                product("qk", e, [(c["wqr"][:, e], ct[:, 0])])
            for e in range(2):
                product("qk", 2 + e, [(c["wkr"][:, k, e], xT[:, k]) for k in range(KD)])
            for e in range(2):
                product("qk", 4 + e, [(c["wuq"][:, e], ct[:, 0])])
            for e in range(2):
                product("qk", 6 + e, [(c["wuk"][:, e], ct[:, 1])])
            pe.wait_ge(sum_step, (KF - 1) * (n + 1))
            u = USES.index("ss")
            wait_for_bank(pe, u, n, first)
            for t in range(NT):
                last = nc.tensor.matmul(bank[u % BANKS][:, t:t + 1], sq_sum[:, t * P:(t + 1) * P],
                                        c["ones"][:, 0:1], start=True, stop=True)
            last.then_inc(mm["ss"], 1)
            if first:
                pe.wait_ge(ternary, 4)
            pe.wait_ge(hlo_ready, KF * (n + 1))
            for t in range(NT):
                product("down", t // 2, [(h_parts[:, i, f, t * P:(t + 1) * P], c["wdn"][:, f]) for f in range(KF)
                                         for i in range(2)], D, (t % 2) * D, t % 2 == 1, t % 2 == 0)
            transposes(n + 1, n, first)
            for t in range(NT):
                product("v", t // 2, [(ct[:, 1, t * P:(t + 1) * P], c["wuv"][:])], D, (t % 2) * D,
                        t % 2 == 1, t % 2 == 0)

        pe.wait_ge(eyes_loaded, 32)
        transposes(0, None, True)
        pe.wait_ge(filled, 1)
        pe.wait_ge(summed, 2)
        nc.tensor.matmul(total[:, 0:2], c["ones"][:], sums[:], start=True, stop=True).then_inc(totalled, 1)
        each_block(pe, body)

    @block.scalar
    def _(act):
        def read_yT(m):
            u = USES.index("yT")
            for k in range(KD):
                act.wait_ge(mm["yT"], 2 * m + k + 1)
                nc.scalar.copy(yT[:, k].rearrange("p a t -> p (a t)"), bank[(u + k) % BANKS][:].bitcast(F16)
                               ).then_inc(rd["yT"], 1)

        def want_table(function):
            nc.scalar.activation(unused[:], c["ones"][0:1, 0:1], function)

        def second_part(name, j, n):
            act.wait_ge(rest_ready, 2 * n + j + 1)
            nc.scalar.copy(part[name][:, 1], rest[name][:]).then_inc(p2_ready, 1)

        def upper_part(m, first):
            act.wait_ge(y_ready, m + 1)
            if not first:
                act.wait_ge(mm["yT"], 2 * m)
            nc.scalar.copy(y_parts[:, 0], y[:]).then_inc(yhi_ready, 1)

        def body(b, n, hf, first):
            for i, bias in enumerate(("bdq", "bdkv")):
                act.wait_ge(mm["ct"], 2 * n + i + 1)
                nc.scalar.activation(ct[:, i], bank[USES.index("ct") + i][:], ACT.Identity, bias=c[bias][:]
                                     ).then_inc(rd["ct"], 1)
            for f in range(KF):
                act.wait_ge(mm["up"], KF * n + f + 1)
                if not first:
                    act.wait_ge(hlo_ready, KF * n - KF + f + 1)
                nc.scalar.activation(h[:, f], bank[(USES.index("up") + f) % BANKS][:], ACT.Gelu
                                     ).then_inc(rd["up"], 1)
                act.wait_ge(rd["up"], KF * n + f + 1)
                if f == 0:
                    nc.scalar.activation(sq_sum[:], h[:, f], ACT.Square).then_inc(sq_ready, 1)
                else:
                    if f > 2:
                        act.wait_ge(sum_step, (KF - 1) * n + f - 2)
                    nc.scalar.activation(sq[:, f % 2], h[:, f], ACT.Square).then_inc(sq_ready, 1)
                if f >= KF - 2:
                    nc.scalar.copy(h_parts[:, 0, f], h[:, f]).then_inc(last_hhi_ready, 1)
            upper_part(n + 1, False)
            want_table(ACT.Silu)
            for j, name in enumerate("qk"):
                act.wait_ge(rd["qk"], 8 * n + 6 + 2 * j)
                if not first:
                    act.wait_ge(parts_stored[name], 96 * n)
                nc.scalar.copy(part[name][:, 0], full[name][:]).then_inc(p1_ready, 1)
            second_part("q", 0, n)
            act.wait_ge(r_ready, n + 1)
            if not isinstance(b, int):
                act.wait_ge(gate_stored[hf], 16 * b)
            for t in range(NT):
                act.wait_ge(mm["down"], 2 * n + t // 2 + 1)
                u = USES.index("down") + t // 2
                nc.scalar.activation(gate[:, hf, t], bank[u % BANKS][:, (t % 2) * D:(t % 2 + 1) * D], ACT.Silu,
                                     scale=ms["r"][:, t:t + 1]).then_inc(rd["down"], 1)
            second_part("k", 1, n)
            want_table(ACT.Gelu)
            read_yT(n + 1)

        upper_part(0, True)
        read_yT(0)
        act.wait_ge(filled, 1)
        act.wait_ge(constants_loaded, CONSTANTS_DONE)
        each_block(act, body)

    @block.vector
    def _(dve):
        def statistics(m, buf, loads):
            dve.wait_ge(x_loaded[buf], 16 * loads)
            for t in range(NT):
                nc.vector.bn_stats(stats[:, t], x_s[:, buf, t]).then_inc(stat_done, 1)
            dve.wait_ge(stat_done, NT * m + NT)
            dve.sem_inc(stats_complete)
            for t in range(NT):
                nc.vector.bn_aggr(mv[:, t], stats[:, t]).then_inc(mv_done, 1)

        def variances(m):
            dve.wait_ge(mv_done, NT * m + NT)
            nc.vector.tensor_copy(ln["var"][:, 0], mv[:, :, 1]).then_inc(var_ready, 1)
            nc.vector.tensor_scalar(ln["var"][:, 1], mv[:, :, 1], LN_EPS, None, ALU.add).then_inc(var_ready, 1)

        def factors(m):
            at = LN_STEPS * m
            dve.wait_ge(roots_ready, m + 1)
            nc.vector.reciprocal(ln["rstd"][:], ln["root"][:, 1]).then_inc(ln_step, 1)
            dve.wait_ge(ln_step, at + 1)
            nc.vector.tensor_tensor(ln["rms"][:], ln["root"][:, 0], ln["rstd"][:], ALU.mult).then_inc(ln_step, 1)
            dve.wait_ge(ln_step, at + 2)
            nc.vector.tensor_scalar(ln["rmse"][:], ln["rms"][:], RMS_EPS, None, ALU.add).then_inc(ln_step, 1)
            dve.wait_ge(ln_step, at + 3)
            nc.vector.reciprocal(ln["r"][:], ln["rmse"][:]).then_inc(ln_step, 1)
            dve.wait_ge(ln_step, at + 4)
            nc.vector.tensor_tensor(ln["c2"][:], ln["rstd"][:], ln["r"][:], ALU.mult).then_inc(ln_step, 1)

        def ternary_weights():
            for i, name in enumerate(raw):
                dve.wait_ge(weights_loaded[name], 16)
                nc.vector.tensor_reduce(sums[:, i:i + 1], raw[name][:], AX.X, ALU.add,
                                        apply_absolute_value=True).then_inc(summed, 1)
            dve.wait_ge(totalled, 1)
            nc.vector.tensor_scalar(limit[:], total[:, 0:2], 0.5 / (D * F), None, ALU.mult).then_inc(limits, 1)
            nc.vector.tensor_scalar(minus_limit[:], total[:, 0:2], -0.5 / (D * F), None, ALU.mult).then_inc(limits, 1)
            dve.wait_ge(limits, 2)
            for i, name in enumerate(raw):
                if i:
                    dve.wait_ge(ternary, 2 * i)
                nc.vector.tensor_scalar(below[:], raw[name][:], minus_limit[:, i:i + 1], None,
                                        ALU.is_lt).then_inc(ternary, 1)
                dve.wait_ge(ternary, 2 * i + 1)
                flat = c[name][:].rearrange("p a b -> p (a b)")
                nc.vector.scalar_tensor_tensor(flat, raw[name][:], limit[:, i:i + 1], below[:], ALU.is_gt,
                                               ALU.subtract).then_inc(ternary, 1)

        def normalise(m, buf, first):
            dve.wait_ge(ln_step, LN_STEPS * m + LN_STEPS)
            if not first:
                dve.wait_ge(mm["xT"], 2 * m)
            for t in range(NT):
                last = nc.vector.tensor_scalar(xn[:, t], x_s[:, buf, t], mv[:, t, 0:1], ln["rstd"][:, t:t + 1],
                                               ALU.subtract, ALU.mult)
            last.then_inc(xn_ready, 1)
            if not first:
                dve.wait_ge(ylo_ready, m)
            for t in range(NT):
                last = nc.vector.tensor_scalar(y[:, t], x_s[:, buf, t], mv[:, t, 0:1], ln["c2"][:, t:t + 1],
                                               ALU.subtract, ALU.mult)
            last.then_inc(y_ready, 1)

        def lower_part(m):
            dve.wait_ge(yhi_ready, m + 1)
            nc.vector.tensor_tensor(y_parts[:, 1], y[:], y_parts[:, 0], ALU.subtract).then_inc(ylo_ready, 1)

        def read_xT(m):
            u = USES.index("xT")
            for k in range(KD):
                dve.wait_ge(mm["xT"], 2 * m + k + 1)
                nc.vector.tensor_copy(xT[:, k], bank[(u + k) % BANKS][:]).then_inc(rd["xT"], 1)

        def split(n, f):
            dve.wait_ge(rd["up"], KF * n + f + 1)
            if f < KF - 2:
                nc.vector.tensor_copy(h_parts[:, 0, f], h[:, f]).then_inc(hhi_ready, 1)
                dve.wait_ge(hhi_ready, (KF - 2) * n + f + 1)
            else:
                dve.wait_ge(last_hhi_ready, 2 * n + f - KF + 3)
            nc.vector.tensor_tensor(h_parts[:, 1, f], h[:, f], h_parts[:, 0, f], ALU.subtract).then_inc(hlo_ready, 1)

        def body(b, n, hf, first):
            for f in range(KF - 2):
                split(n, f)
                if f == XN_AFTER:
                    normalise(n + 1, (hf + 1) % 2, False)
            tokens = slice(hf * BT, (hf + 1) * BT)
            u = USES.index("qk")
            for j, (name, bias) in enumerate((("q", "bqr"), ("k", "bkr"))):
                if not first:
                    dve.wait_ge(rope_ready, 4 * n - 2 + 2 * j)
                for e in range(2):
                    i = 2 * j + e
                    dve.wait_ge(mm["qk"], 8 * n + i + 1)
                    ps = bank[(u + i) % BANKS][:]
                    b_ = c[bias][:, e:e + 1]
                    nc.vector.scalar_tensor_tensor(rot[name][:, 2 * e], ps, b_, c["cos" if e == 0 else "sin"][:, tokens],
                                                   ALU.add, ALU.mult)
                    nc.vector.scalar_tensor_tensor(rot[name][:, 2 * e + 1], ps, b_,
                                                   c["sin" if e == 0 else "cos"][:, tokens], ALU.add, ALU.mult
                                                   ).then_inc(rd["qk"], 1)
                if j == 0:
                    split(n, KF - 2)
                    split(n, KF - 1)
            for j, (name, bias) in enumerate((("q", "buq"), ("k", "buk"))):
                if not first:
                    dve.wait_ge(rest_ready, 2 * n - 1 + j)
                for e in range(2):
                    i = 4 + 2 * j + e
                    dve.wait_ge(mm["qk"], 8 * n + i + 1)
                    dve.wait_ge(rope_ready, 4 * n + 2 * j + e + 1)
                    nc.vector.scalar_tensor_tensor(full[name][:, e], bank[(u + i) % BANKS][:], c[bias][:, e:e + 1],
                                                   rope[name][:, e], ALU.add, ALU.add).then_inc(rd["qk"], 1)
            lower_part(n + 1)
            dve.wait_ge(mm["ss"], n + 1)
            nc.vector.tensor_scalar(ms["mean"][:], bank[USES.index("ss") % BANKS][:, 0:NT], 1.0 / F, None, ALU.mult
                                    ).then_inc(rd["ss"], 1)
            statistics(n + 2, hf, b + 2)
            variances(n + 2)
            dve.wait_ge(rms_ready, n + 1)
            nc.vector.tensor_scalar(ms["rmse"][:], ms["rms"][:], RMS_EPS, None, ALU.add).then_inc(rmse_ready, 1)
            dve.wait_ge(rmse_ready, n + 1)
            if not first:
                dve.wait_ge(rd["down"], NT * n)
            nc.vector.reciprocal(ms["r"][:], ms["rmse"][:]).then_inc(r_ready, 1)
            read_xT(n + 1)
            for t in range(NT):
                if t == 0 and not isinstance(b, int):
                    dve.wait_ge(v_stored[hf], 16 * b)
                dve.wait_ge(mm["v"], 2 * n + t // 2 + 1)
                ps = bank[(USES.index("v") + t // 2) % BANKS][:, (t % 2) * D:(t % 2 + 1) * D]
                nc.vector.tensor_tensor(vx[:, hf, t, :, 0:HD], ps.rearrange("p (h c) -> p h c", c=HD),
                                        c["buv"][:].rearrange("p (h c) -> p h c", c=HD), ALU.add
                                        ).then_inc(rd["v"], 1)
            factors(n + 2)

        nc.vector.memset(c["ones"][:], 1.0).then_inc(filled, 1)
        statistics(0, 0, 1)
        variances(0)
        factors(0)
        normalise(0, 0, True)
        lower_part(0)
        read_xT(0)
        ternary_weights()
        statistics(1, 1, 1)
        variances(1)
        factors(1)
        dve.wait_ge(constants_loaded, CONSTANTS_DONE)
        dve.wait_ge(vx_filled, 1)
        each_block(dve, body)

    @block.gpsimd
    def _(pool):
        def roots(m):
            pool.wait_ge(var_ready, 2 * m + 2)
            nc.gpsimd.tensor_tensor(ln["root"][:], ln["var"][:], c["halfs"][:], ALU.pow).then_inc(roots_ready, 1)

        def body(b, n, hf, first):
            for f in range(1, KF):
                pool.wait_ge(sq_ready, KF * n + f + 1)
                if f > 1:
                    pool.wait_ge(sum_step, (KF - 1) * n + f - 1)
                nc.gpsimd.tensor_tensor(sq_sum[:], sq_sum[:], sq[:, f % 2], ALU.add).then_inc(sum_step, 1)
            for j, name in enumerate("qk"):
                r = rot[name]
                pool.wait_ge(rd["qk"], 8 * n + 2 * j + 2)
                if not first:
                    pool.wait_ge(p1_ready, 2 * n)
                nc.gpsimd.tensor_tensor(rope[name][:, 0], r[:, 0], r[:, 2], ALU.subtract).then_inc(rope_ready, 1)
                nc.gpsimd.tensor_tensor(rope[name][:, 1], r[:, 3], r[:, 1], ALU.add).then_inc(rope_ready, 1)
            for j, name in enumerate("qk"):
                if j:
                    pool.wait_ge(rd["ss"], n + 1)
                    nc.gpsimd.tensor_tensor(ms["rms"][:], ms["mean"][:], c["halfs"][:, 0], ALU.pow
                                            ).then_inc(rms_ready, 1)
                pool.wait_ge(p1_ready, 2 * n + j + 1)
                if not first:
                    pool.wait_ge(p3_ready, 2 * n - 1 + j)
                nc.gpsimd.tensor_tensor(rest[name][:], full[name][:], part[name][:, 0], ALU.subtract
                                        ).then_inc(rest_ready, 1)
            for j, name in enumerate("qk"):
                pool.wait_ge(p2_ready, 2 * n + j + 1)
                nc.gpsimd.tensor_tensor(part[name][:, 2], rest[name][:], part[name][:, 1], ALU.subtract
                                        ).then_inc(p3_ready, 1)
                if j == 0:
                    roots(n + 2)

        nc.gpsimd.memset(c["halfs"][:], 0.5).then_inc(halfs_filled, 1)
        pool.wait_ge(halfs_filled, 1)
        roots(0)
        nc.gpsimd.memset(vx[:], 1.0).then_inc(vx_filled, 1)
        roots(1)
        each_block(pool, body)


def attend(nc, semaphore, ctx, exact, repeat, B, x, wo, bo, parts_d, v_d, gate_d, negmax_d, den_d, rden_d, out):
    suffix = "_exact" if exact else ""

    def sem(name):
        return semaphore(name + suffix)

    def sb(name, shape, dt=F32):
        return ctx.enter_context(nc.sbuf_tensor(name + suffix, shape, dt))

    CHUNK = P
    CHUNKS = S // CHUNK if exact else 1
    stack = {n: sb(f"stack_{n}", [ROWS + 1, NG, GH, S], BF16) for n in "qk"}
    v_s = sb("v_s", [P, NG, KT, GH, 2 * HD])
    probs = sb("probs", [P, 2, GH, BT])
    maxima = sb("maxima", [P, 2, GH * QT, CHUNKS])
    negmax = sb("negmax_s", [P, 2, GH * QT], BF16)
    negmax_t = sb("negmax_t", [P, 2, GH * QT], BF16)
    raw = sb("raw", [P, 2, S])
    o = sb("o", [P, KD, S])
    o_over = sb("o_over", [P, KD, S])
    den = sb("den_s", [P, P])
    rden = sb("rden_s", [P, P])
    rden_b = sb("rden_b", [P, KD, S])
    wo_s = sb("wo_s", [P, KD, D])
    bo_s = sb("bo_s", [P, D])
    res = sb("res", [P, 2, NT, D])
    x_r = sb("x_r", [P, 2, NT, D])
    gate_r = sb("gate_r", [P, 2, NT, D])
    scores = ctx.enter_context(nc.psum_tensor("scores" + suffix, [P, RING, 2, BT], F32))
    shared = ctx.enter_context(nc.psum_tensor("shared" + suffix, [P, BT], F32))
    for_max, projected = shared[:, 0:D], shared[:, D:2 * D]
    sums = ctx.enter_context(nc.psum_tensor("sums" + suffix, [P, BT], F32))

    loaded2, ones_set = sem("wo_loaded"), sem("ones_set")
    stack_loaded = [sem(f"stack_loaded{g}") for g in range(NG)]
    shift_ones_loaded = sem("shift_ones_loaded")
    st_full, exp_done, pv_done, evacuated = sem("st_full"), sem("exp_done"), sem("pv_done"), sem("evacuated")
    max_full, max_free = sem("max_full"), sem("max_free")
    negmax_ready, negmax_turned = sem("negmax_ready"), sem("negmax_turned")
    negmax_out, shift_loaded = sem("negmax_out"), sem("shift_loaded")
    heads_placed = [sem(f"heads_placed{i}") for i in range(2)]
    den_loaded = sem("den_loaded")
    rden_ready, rden_out, rden_loaded = sem("rden_ready"), sem("rden_out"), sem("rden_loaded")
    o_ready, y_full, y_free, res_step = sem("o_ready"), sem("y_full"), sem("y_free"), sem("res_step")
    sync_passed = sem("sync_passed")
    xg_loaded, out_stored = sem("xg_loaded"), sem("out_stored")
    pool_passed = sem("pool_passed")
    out_free = sem("out_free")
    STACK_DMAS = 2 * len(TERMS) + 1
    INVERT_AT, NORMALISE_AT = 6, (12, 14)
    UNIT = HEAD_TILES * CHUNKS if exact else 1
    SK = S // SAMPLE
    TILES = S // P
    within = sb("within", [P, P])
    fine = sb("fine", [P, 2])
    over = sb("over", [P, 1])
    ones = sb("ones_2", [P, P])
    ones_row = sb("ones_row", [P, NG * GH * S // P], BF16)
    fine_step, over_ready, over_total = sem("fine_step"), sem("over_ready"), sem("over_total")
    repeat_ready = sem("repeat_ready")

    def when_wanted(eng, program):
        if exact:
            with eng.If(eng.value_load(repeat[0:1, 0:1], min_val=0, max_val=P) > 0):
                program()
        else:
            program()

    block = ctx.enter_context(nc.Block())

    def ahead(g, s):
        u = g * STEPS + s + LEAD
        return u // (NG * STEPS), (u // STEPS) % NG, u % STEPS

    def slot(g, s, i):
        return ((g * STEPS + s) * 2 + i) % RING

    def spare(n):
        return scores[:, n % (2 * RING) // 2, n % 2]

    def previous(b, g, s):
        return (b, g, s - 1) if s else ((b, g - 1, STEPS - 1) if g else (b - 1, NG - 1, STEPS - 1))

    def rounds(eng_Fori, T, O_after):
        T(0, 0, B == 1)
        T(0, 1, B == 1)
        if B > 1:
            with eng_Fori(0, B - 1) as b:
                T(b, 2, False)
                T(b, 3, False)
                T(b + 1, 0, False)
                T(b + 1, 1, False)
                O_after(b)
        T(B - 1, 2, True)
        T(B - 1, 3, True)

    @block.sync
    def _(sp):
        def wait(what, value):
            sp.wait_ge(what, value)
            sp.sem_inc(sync_passed)

        def load_group(b, g):
            for k, name in enumerate("qk"):
                for t, pair in enumerate(TERMS):
                    rows = parts_d[name][b, pair[k], g * GH * HD:(g + 1) * GH * HD, :]
                    sp.dma_start(stack[name][t * HD:(t + 1) * HD, g], rows.rearrange("(j i) t -> i j t", i=HD)
                                 ).then_inc(stack_loaded[g], 16)
            sp.dma_start(v_s[:, g], v_d[b, :, g * GH:(g + 1) * GH, :].rearrange("(k p) j c -> p k j c", p=P)
                         ).then_inc(stack_loaded[g], 16)

        def place_heads(b, g):
            wait(evacuated, 2 * (b * NG + g + 1))
            if g == 0 and not isinstance(b, int):
                wait(o_ready, KD * b)
            for j in range(GH):
                head = g * GH + j
                at = (head * HD) % P
                sp.dma_start(o[at:at + HD, head * HD // P], raw[32 * j:32 * j + HD, g % 2]
                             ).then_inc(heads_placed[g % 2], 16)
            sp.dma_start(den_d[g * GH:(g + 1) * GH, :], raw[HD:P:32, g % 2]).then_inc(heads_placed[g % 2], 16)

        def load_denominators(b):
            for placed in heads_placed:
                wait(placed, 40 * NG * b + 40 * NG)
            sp.dma_start(den[:], den_d.rearrange("h (a c) -> (h a) c", c=P)).then_inc(den_loaded, 16)

        def spread_denominators(b):
            wait(rden_ready, b + 1)
            sp.dma_start(rden_d.rearrange("h (a c) -> (h a) c", c=P), rden[:]).then_inc(rden_out, 16)
            wait(rden_out, 16 * b + 16)
            for i in range(P // HD):
                sp.dma_start(rden_b[i * HD:(i + 1) * HD], rden_d.rearrange("(k h) t -> h k t", k=KD)[i]
                             .partition_broadcast(HD)).then_inc(rden_loaded, 16)

        def load_residual(b):
            for k in range(2):
                tokens = slice(k * BT, (k + 1) * BT)
                sp.dma_start(x_r[:, k], x[b, tokens].rearrange("(t p) d -> p t d", p=P)).then_inc(xg_loaded, 16)
                sp.dma_start(gate_r[:, k], gate_d[b, tokens].rearrange("(t p) d -> p t d", p=P)
                             ).then_inc(xg_loaded, 16)

        def T(b, g, last):
            first = isinstance(b, int) and b == 0 and g == 0
            G = b * NG + g
            if g == 0 and not first:
                place_heads(b - 1, NG - 1)
                load_denominators(b - 1)
                spread_denominators(b - 1)
            if g >= 2 and not last:
                wait(st_full, 2 * STEPS * G)
                wait(pv_done, STEPS * G)
                load_group(b + 1, g - 2)
            if g:
                place_heads(b, g - 1)
            if g == NG - 1:
                load_residual(b)
                if not last:
                    load_group(b + 1, 2)
            if g == 0:
                if not first:
                    wait(st_full, 2 * STEPS * G)
                    wait(pv_done, STEPS * G)
                load_group(b, 3)

        def O(b):
            for k in range(2):
                wait(res_step, 2 * (TILES * b + (k + 1) * NT))
                sp.dma_start(out[b, k * BT:(k + 1) * BT].rearrange("(t p) d -> p t d", p=P), res[:, k]
                             ).then_inc(out_stored, 16)

        def program():
            sp.dma_start(wo_s[:], wo.rearrange("(k p) n -> p k n", p=P)).then_inc(loaded2, 16)
            sp.dma_start(bo_s[:], bo.partition_broadcast(P)).then_inc(loaded2, 16)
            for g in range(3):
                load_group(0, g)
                if g == 0:
                    wait(ones_set, 1)
                    sp.dma_start(stack["k"][ROWS:ROWS + 1].rearrange("p g j t -> p (g j t)"), ones_row[:]
                                 ).then_inc(shift_ones_loaded, 16)
            rounds(sp.Fori, T, O)
            place_heads(B - 1, NG - 1)
            load_denominators(B - 1)
            spread_denominators(B - 1)
            O(B - 1)
            wait(out_stored, 32 * B)
            for g in range(NG):
                wait(stack_loaded[g], 16 * STACK_DMAS * B)

        when_wanted(sp, program)

    @block.tensor
    def _(pe):
        def wait_for_stack(b, g, u):
            if u == 0:
                pe.wait_ge(stack_loaded[g], b * 16 * STACK_DMAS + 16 * STACK_DMAS)

        def maxima_products(b, g, u, t, region=for_max, regions=1):
            j, qt = u * HEAD_TILES // QT, u * HEAD_TILES % QT + t
            base = (b * NG + g) * STEPS * UNIT + u * UNIT
            queries = stack["q"][0:ROWS, g, j, qt * P:(qt + 1) * P]
            if exact:
                for c in range(CHUNKS):
                    index = base + CHUNKS * t + c
                    if not (isinstance(index, int) and index == 0):
                        pe.wait_ge(max_free, index)
                    nc.tensor.matmul(for_max[:, 0:CHUNK], queries, stack["k"][0:ROWS, g, j, c * CHUNK:(c + 1) * CHUNK],
                                     start=True, stop=True).then_inc(max_full, 1)
            else:
                if t == 0 and not (isinstance(base, int) and base < regions):
                    pe.wait_ge(max_free, base + 1 - regions)
                mm = nc.tensor.matmul(region[:, t * SK:(t + 1) * SK], queries,
                                      stack["k"][0:ROWS, g, j, 0:S:SAMPLE], start=True, stop=True)
                if t == HEAD_TILES - 1:
                    mm.then_inc(max_full, 1)

        def pv(b, g, s):
            n = (b * NG + g) * STEPS + s
            pe.wait_ge(exp_done, 2 * n + 2)
            if s % KT == 0 and not (isinstance(n, int) and n == 0):
                pe.wait_ge(evacuated, 2 * (b * NG + g) + s // KT)
            for j in range(GH):
                last = nc.tensor.matmul(sums[32 * j:32 * j + 32], v_s[:, g, s % KT, j], probs[:, s % 2, j],
                                        start=(s % KT == 0), stop=(s % KT == KT - 1))
            last.then_inc(pv_done, 1)

        def project_tile(b, t, region=projected):
            pe.wait_ge(o_ready, KD * b + KD)
            for i in range(KD):
                mm = nc.tensor.matmul(region, o_over[:, i, t * P:(t + 1) * P], wo_s[:, i],
                                      start=(i == 0), stop=(i == KD - 1))
            mm.then_inc(y_full, 1)

        def T(b, g, last):
            G = b * NG + g
            first = isinstance(b, int) and b == 0 and g == 0
            after_first = not (isinstance(b, int) and b == 0)
            pe.wait_ge(shift_loaded, 16 * G + 16)
            for s in range(STEPS):
                db, mg, u = ahead(g, s)
                more = not (last and db)
                queries = slice(s // KT * BT, (s // KT + 1) * BT)
                if more:
                    wait_for_stack(b + db, mg, u)
                for i in range(2):
                    e = (G * STEPS + s) * 2 + i
                    if not (first and 2 * s + i < RING):
                        pe.wait_ge(exp_done, e - 1 if g == 0 and 2 * s + i < 2 else e + 1 - RING)
                    for j in range(2):
                        mm = nc.tensor.matmul(scores[:, slot(g, s, i), j],
                                              stack["k"][:, g, 2 * i + j, s % KT * P:(s % KT + 1) * P],
                                              stack["q"][:, g, 2 * i + j, queries], start=True, stop=True)
                    mm.then_inc(st_full, 1)
                if more:
                    if after_first and ((g == 1 and s and s % 2 == 0) or (g == 2 and s == 0)):
                        pe.wait_ge(y_free, TILES * (b - 1) + (s // 2 or TILES))
                    for t in range(HEAD_TILES):
                        maxima_products(b + db, mg, u, t)
                if not (first and s == 0):
                    pv(*previous(b, g, s))
                if g == 1 and s % 2 == 1 and after_first:
                    pe.wait_ge(max_free, ((b + db) * NG + mg) * STEPS * UNIT + (u + 1) * UNIT)
                    project_tile(b - 1, s // 2)

        def program():
            pe.wait_ge(loaded2, 32)
            for n in range(LEAD):
                wait_for_stack(0, n // STEPS, n % STEPS)
                for t in range(HEAD_TILES):
                    maxima_products(0, n // STEPS, n % STEPS, t, *(() if exact else (spare(n), 2 * RING)))
            pe.wait_ge(ones_set, 2)
            pe.wait_ge(shift_ones_loaded, 16)
            pe.wait_ge(max_free, LEAD * UNIT)
            rounds(pe.Fori, T, lambda b: None)
            pv(B - 1, NG - 1, STEPS - 1)
            for t in range(TILES):
                if t >= 2 * RING:
                    pe.wait_ge(y_free, TILES * (B - 1) + t + 1 - 2 * RING)
                project_tile(B - 1, t, spare(t)[:, 0:D])
            if not exact:
                pe.wait_ge(over_ready, 1)
                nc.tensor.matmul(for_max[:, 0:1], ones[:], over[:], start=True, stop=True).then_inc(over_total, 1)

        when_wanted(pe, program)

    @block.scalar
    def _(act):
        def T(b, g, last):
            G = b * NG + g
            first = isinstance(b, int) and b == 0 and g == 0
            for s in range(STEPS):
                n = G * STEPS + s
                for i in range(2):
                    act.wait_ge(st_full, 2 * n + i + 1)
                    if i == 0 and not (first and s < 2):
                        act.wait_ge(pv_done, n - 1)
                    nc.scalar.activation(probs[:, s % 2, 2 * i:2 * i + 2], scores[:, slot(g, s, i)], ACT.Exp,
                                         scale=SCORE_SCALE).then_inc(exp_done, 1)

        when_wanted(act, lambda: rounds(act.Fori, T, lambda b: None))

    @block.vector
    def _(dve):
        def reduce_unit(b, g, u, region=for_max):
            G, par = b * NG + g, g % 2
            for i in range(UNIT):
                dve.wait_ge(max_full, G * STEPS * UNIT + u * UNIT + i + 1)
                if exact:
                    nc.vector.tensor_reduce(maxima[:, par, u * HEAD_TILES + i // CHUNKS, i % CHUNKS:i % CHUNKS + 1],
                                            for_max[:, 0:CHUNK], AX.X, ALU.max).then_inc(max_free, 1)
                else:
                    nc.vector.tensor_reduce(maxima[:, par, u * HEAD_TILES:(u + 1) * HEAD_TILES, 0],
                                            region[:, 0:HEAD_TILES * SK].rearrange(
                                                "p (t k) -> p t k", t=HEAD_TILES), AX.X, ALU.max
                                            ).then_inc(max_free, 1)
            if u == STEPS - 1:
                dve.wait_ge(max_free, (G + 1) * STEPS * UNIT)
                if exact:
                    nc.vector.tensor_reduce(negmax[:, par], maxima[:, par], AX.X, ALU.max, negate=True
                                            ).then_inc(negmax_ready, 1)
                else:
                    nc.vector.tensor_scalar(negmax[:, par], maxima[:, par, :, 0], -1.0, -HEADROOM / SCORE_SCALE,
                                            ALU.mult, ALU.add).then_inc(negmax_ready, 1)
                dve.wait_ge(negmax_ready, G + 1)
                if not (isinstance(b, int) and b == 0 and g < 2):
                    dve.wait_ge(negmax_out, 64 * G - 64)
                nc.vector.transpose(negmax_t[:, par], negmax[:, par]).then_inc(negmax_turned, 1)

        def evacuate(b, g, half):
            dve.wait_ge(pv_done, (b * NG + g) * STEPS + (half + 1) * KT)
            if g >= 2 and half == 0:
                dve.wait_ge(heads_placed[g % 2], 40 * NG * b + 80)
            nc.vector.tensor_copy(raw[:, g % 2, half * BT:(half + 1) * BT], sums[:]).then_inc(evacuated, 1)

        def invert(b):
            dve.wait_ge(den_loaded, 16 * b + 16)
            nc.vector.reciprocal(rden[:], den[:]).then_inc(rden_ready, 1)
            if not exact:
                nc.vector.tensor_scalar(within[:], den[:], DEN_LIMIT, None, ALU.is_le).then_inc(fine_step, 1)
                dve.wait_ge(fine_step, 3 * b + 2)
                nc.vector.tensor_reduce(fine[:, 1:2], within[:], AX.X, ALU.min).then_inc(fine_step, 1)
                dve.wait_ge(fine_step, 3 * b + 3)
                nc.vector.tensor_tensor(fine[:, 0:1], fine[:, 0:1], fine[:, 1:2], ALU.min).then_inc(fine_step, 1)

        def normalise(b, i):
            dve.wait_ge(rden_loaded, 16 * (P // HD) * b + 16 * (P // HD))
            nc.vector.tensor_tensor(o_over[:, i], o[:, i], rden_b[:, i], ALU.mult).then_inc(o_ready, 1)

        def read_tile(b, t, region=projected):
            k, at = t // NT, 2 * (TILES * b + t)
            r = res[:, k, t % NT]
            if t == 0:
                dve.wait_ge(out_free, b + 1)
            dve.wait_ge(y_full, TILES * b + t + 1)
            nc.vector.tensor_tensor(r, region, bo_s[:], ALU.add).then_inc(y_free, 1)
            if t == 0:
                dve.wait_ge(xg_loaded, 64 * b + 64)
            dve.wait_ge(y_free, TILES * b + t + 1)
            nc.vector.tensor_tensor(r, r, gate_r[:, k, t % NT], ALU.mult).then_inc(res_step, 1)
            dve.wait_ge(res_step, at + 1)
            nc.vector.tensor_tensor(r, r, x_r[:, k, t % NT], ALU.add).then_inc(res_step, 1)

        def T(b, g, last):
            first = isinstance(b, int) and b == 0 and g == 0
            for s in range(STEPS):
                db, mg, u = ahead(g, s)
                if not (last and db):
                    reduce_unit(b + db, mg, u)
                if s == KT:
                    evacuate(b, g, 0)
                if s == 0 and not first:
                    evacuate(*((b, g - 1) if g else (b - 1, NG - 1)), 1)
                if g == 0 and not first:
                    if s == INVERT_AT:
                        invert(b - 1)
                    if s in NORMALISE_AT:
                        normalise(b - 1, NORMALISE_AT.index(s))
                if g == 1 and s % 2 == 1 and not (isinstance(b, int) and b == 0):
                    read_tile(b - 1, s // 2)

        def program():
            nc.vector.memset(ones_row[:], 1.0).then_inc(ones_set, 1)
            nc.vector.memset(ones[:], 1.0).then_inc(ones_set, 1)
            nc.vector.memset(fine[:], 1.0).then_inc(fine_step, 1)
            for n in range(LEAD):
                reduce_unit(0, n // STEPS, n % STEPS, *(() if exact else (spare(n),)))
            dve.wait_ge(loaded2, 32)
            rounds(dve.Fori, T, lambda b: None)
            evacuate(B - 1, NG - 1, 1)
            invert(B - 1)
            for i in range(KD):
                normalise(B - 1, i)
            for t in range(TILES):
                read_tile(B - 1, t, spare(t)[:, 0:D])
            if not exact:
                dve.wait_ge(fine_step, 3 * B + 1)
                nc.vector.tensor_scalar(over[:], fine[:, 0:1], 0.5, None, ALU.is_lt).then_inc(over_ready, 1)
                dve.wait_ge(over_total, 1)
                nc.vector.tensor_copy(repeat[:], for_max[:, 0:1]).then_inc(repeat_ready, 1)

        when_wanted(dve, program)

    @block.gpsimd
    def _(pool):
        def wait(what, value):
            pool.wait_ge(what, value)
            pool.sem_inc(pool_passed)

        def shift_rows(b, g):
            G, par = b * NG + g, g % 2
            wait(negmax_turned, G + 1)
            for q in range(4):
                pool.dma_start(negmax_d[par].rearrange("(c q r) -> q c r", q=4, r=32)[q],
                             negmax_t[32 * q:32 * q + 32, par, :]).then_inc(negmax_out, 16)
            wait(negmax_out, G * 64 + 64)
            pool.dma_start(stack["q"][ROWS:ROWS + 1, g].rearrange("p j t -> p (j t)"), negmax_d[par:par + 1, :]
                         ).then_inc(shift_loaded, 16)

        def T(b, g, last):
            if g < NG - 1:
                shift_rows(b, g + 1)
            elif not last:
                shift_rows(b + 1, 0)

        def O(b):
            wait(out_stored, 32 * b + 32)
            pool.sem_inc(out_free)

        def program():
            pool.sem_inc(out_free)
            shift_rows(0, 0)
            rounds(pool.Fori, T, O)
            O(B - 1)

        when_wanted(pool, program)


_NAMES = ["x", "wdq", "bdq", "wdkv", "bdkv", "wuq", "buq", "wqr", "bqr", "wkr", "bkr", "wuk", "buk", "wuv", "buv",
          "wo", "bo", "wup", "wdn", "cos", "sin", "eye32", "eye16"]


def lay_out(i):
    def eo(w):
        return np.ascontiguousarray(w.reshape(w.shape[0], D // 2, 2).transpose(0, 2, 1))

    def col(v):
        return np.ascontiguousarray(v.reshape(-1, 1))

    def pair(v):
        return np.ascontiguousarray(v.reshape(D // 2, 2))

    a = {k: np.asarray(v) for k, v in i.items()}
    f = lambda name: a["L0_attn_" + name]
    position = np.arange(S, dtype=np.float32)[:, None]
    ids = np.arange(D // 2, dtype=np.float32)
    theta = (np.float32(10000.0) ** (np.float32(-2.0) * ids)) / np.float32(D // 2)
    angle = (position * theta[None, :]).astype(np.float32)
    return {
        "x": f("x"), "wdq": f("Wd_q_w"), "bdq": col(f("Wd_q_b")), "wdkv": f("Wd_kv_w"), "bdkv": col(f("Wd_kv_b")),
        "wuq": eo(f("Wu_q_w")), "buq": pair(f("Wu_q_b")), "wqr": eo(f("Wq_r_w")), "bqr": pair(f("Wq_r_b")),
        "wkr": eo(f("Wk_r_w")), "bkr": pair(f("Wk_r_b")), "wuk": eo(f("Wu_k_w")), "buk": pair(f("Wu_k_b")),
        "wuv": f("Wu_v_w"), "buv": f("Wu_v_b"), "wo": f("Wo_w"), "bo": f("Wo_b"),
        "wup": np.ascontiguousarray(a["L0_ffn_w_up"].T), "wdn": np.ascontiguousarray(a["L0_ffn_w_down"].T),
        "cos": np.ascontiguousarray(np.cos(angle).T), "sin": np.ascontiguousarray(np.sin(angle).T),
        "eye32": np.eye(P, dtype=np.float32), "eye16": np.eye(P, dtype=np.float16),
    }


def kernel(**inputs):
    import concourse.bacc as bacc
    from concourse.bass_utils import run_bass_kernel_spmd as run

    nc = bacc.Bacc("TRN2", target_bir_lowering=False, num_devices=1)
    laid = lay_out(inputs)
    arrays = {f"in_{n}": np.ascontiguousarray(laid[n]) for n in _NAMES}
    args = [nc.dram_tensor(f"in_{n}", arrays[f"in_{n}"].shape, mybir.dt.from_np(arrays[f"in_{n}"].dtype),
                           kind="ExternalInput").ap() for n in _NAMES]
    out = nc.dram_tensor("out_0", laid["x"].shape, F32, kind="ExternalOutput").ap()
    build_program(nc, *args, out)
    r = run(nc, [arrays], core_ids=[0])
    return r.results[0]["out_0"]
```
